# Optimizing a Trainium2 kernel written in Bass

```python
import numpy as np
import jax
import jax.numpy as jnp

def _softmax(x, axis=-1):
    return jax.nn.softmax(x, axis=axis)

def _gelu(x):
    return jax.nn.gelu(x, approximate=True)

def _silu(x):
    return jax.nn.silu(x)

def _sigmoid(x):
    return jax.nn.sigmoid(x)

def _layernorm(x, axis=-1, eps=1e-05):
    m = jnp.mean(x, axis=axis, keepdims=True)
    v = jnp.var(x, axis=axis, keepdims=True)
    return (x - m) / jnp.sqrt(v + eps)

def _scatter_add(tgt, idx, src, axis=0):
    return tgt.at[idx].add(src)

def _segment_sum(src, seg, n):
    return jax.ops.segment_sum(src, seg, n)
kernel_name = 'mk_vit_tower_cls_d2_tok_img256_r4_fed615'

def setup_inputs(seed: int=0):
    np.random.seed(seed)
    _w = jnp.asarray

    def _rec_inputs():
        import jax
        import jax.numpy as jnp
        _rk = jax.random.key(seed)
        x = -7.10856e-05 + 0.999911 * jax.random.normal(jax.random.fold_in(_rk, 1), (8, 64, 128, 64), jnp.float32)
        cls_tok = 0.02 * jax.random.normal(jax.random.fold_in(_rk, 5), (1, 1, 64), jnp.float32)
        return (x, cls_tok)
    x, cls_tok = _rec_inputs()

    def _L0_tok_setup():
        import jax, jax.numpy as jnp
        import numpy as np
        PATCH_LEN = 16
        STRIDE = 8
        PAD = 8
        key = jax.random.key(seed)
        k1, k2 = jax.random.split(key)
        x = jax.random.normal(k1, (32, 64, 128, 64), dtype=jnp.float32)
        in_feat = 64 * (PATCH_LEN // 2 + 1) * 2
        W = jax.random.normal(k2, (64, in_feat), dtype=jnp.float32) * 0.02
        return {'x': x, 'W': W}
    _L0_tok_all = _L0_tok_setup()
    _L0_tok_in = {k: v for k, v in _L0_tok_all.items() if k in ('W',)}
    del _L0_tok_all

    def _L0_attn_setup():
        import jax, jax.numpy as jnp
        import numpy as np
        GAMMA = 0.96875
        ROPE_THETA = 10000.0

        def _rope(x):
            B, S, d = x.shape
            inv_freq = 1.0 / ROPE_THETA ** (jnp.arange(0, d, 2, dtype=jnp.float32) / d)
            angles = jnp.arange(S, dtype=jnp.float32)[:, None] * inv_freq[None, :]
            cos = jnp.cos(angles).astype(x.dtype)
            sin = jnp.sin(angles).astype(x.dtype)
            xs = x.reshape(B, S, d // 2, 2)
            x0, x1 = (xs[..., 0], xs[..., 1])
            out = jnp.stack([x0 * cos - x1 * sin, x1 * cos + x0 * sin], axis=-1)
            return out.reshape(B, S, d)

        def _decay_mask(S, dtype):
            n = jnp.arange(S)[:, None]
            m = jnp.arange(S)[None, :]
            diff = n - m
            D = jnp.exp(jnp.maximum(diff, 0).astype(jnp.float32) * np.log(GAMMA))
            return jnp.where(diff >= 0, D, 0.0).astype(dtype)
        key = jax.random.key(seed)
        k1, k2, k3, k4 = jax.random.split(key, 4)
        H = 64
        X = jax.random.normal(k1, (4, 2048, H), dtype=jnp.float32)
        W_Q = jax.random.normal(k2, (H, H), dtype=jnp.float32) / H
        W_K = jax.random.normal(k3, (H, H), dtype=jnp.float32) / H
        W_V = jax.random.normal(k4, (H, H), dtype=jnp.float32) / H
        return {'X': X, 'W_Q': W_Q, 'W_K': W_K, 'W_V': W_V}
    _L0_attn_all = _L0_attn_setup()
    _L0_attn_in = {k: v for k, v in _L0_attn_all.items() if k in ('W_Q', 'W_K', 'W_V')}
    del _L0_attn_all

    def _L0_ffn_setup():
        import jax, jax.numpy as jnp
        import numpy as np
        B, S, H, F, E, K = (8, 1024, 64, 128, 16, 2)
        EPS = 1e-05
        key = jax.random.key(seed)
        ks = jax.random.split(key, 9)
        sc = 0.02
        return {'x': jax.random.normal(ks[0], (B, S, H), dtype=jnp.float32), 'gate_w': jax.random.normal(ks[1], (H, E), dtype=jnp.float32) * sc, 'gate_b': jnp.zeros((E,), dtype=jnp.float32), 'w1': jax.random.normal(ks[2], (E, H, F), dtype=jnp.float32) * sc, 'b1': jnp.zeros((E, F), dtype=jnp.float32), 'w2': jax.random.normal(ks[3], (E, F, H), dtype=jnp.float32) * sc, 'b2': jnp.zeros((E, H), dtype=jnp.float32), 'gamma': jnp.ones((H,), dtype=jnp.float32), 'beta': jnp.zeros((H,), dtype=jnp.float32)}
    _L0_ffn_all = _L0_ffn_setup()
    _L0_ffn_in = {k: v for k, v in _L0_ffn_all.items() if k in ('gate_w', 'gate_b', 'w1', 'b1', 'w2', 'b2', 'gamma', 'beta')}
    del _L0_ffn_all

    def _L1_attn_setup():
        import jax, jax.numpy as jnp
        import numpy as np
        MIDC = 64
        HEADS = 16
        HEADC = MIDC // HEADS
        EPS = 1e-05

        def _layernorm(x, w, b):
            mean = jnp.mean(x, axis=-1, keepdims=True)
            std = jnp.std(x, axis=-1, keepdims=True, ddof=1)
            return w * (x - mean) / (std + EPS) + b
        key = jax.random.key(seed)
        ks = jax.random.split(key, 3)
        B, HW = (8, 4096)
        x = jax.random.normal(ks[0], (B, HW, MIDC), dtype=jnp.float32)
        W_qkv = jax.random.normal(ks[1], (3 * MIDC, MIDC), dtype=jnp.float32) * 0.02
        b_qkv = jnp.zeros((3 * MIDC,), dtype=jnp.float32)
        kln_w = jnp.ones((HEADS, 1, HEADC), dtype=jnp.float32)
        kln_b = jnp.zeros((HEADS, 1, HEADC), dtype=jnp.float32)
        vln_w = jnp.ones((HEADS, 1, HEADC), dtype=jnp.float32)
        vln_b = jnp.zeros((HEADS, 1, HEADC), dtype=jnp.float32)
        W_proj = jax.random.normal(ks[2], (MIDC, MIDC), dtype=jnp.float32) * 0.02
        b_proj = jnp.zeros((MIDC,), dtype=jnp.float32)
        return {'x': x, 'W_qkv': W_qkv, 'b_qkv': b_qkv, 'kln_w': kln_w, 'kln_b': kln_b, 'vln_w': vln_w, 'vln_b': vln_b, 'W_proj': W_proj, 'b_proj': b_proj}
    _L1_attn_all = _L1_attn_setup()
    _L1_attn_in = {k: v for k, v in _L1_attn_all.items() if k in ('W_qkv', 'b_qkv', 'kln_w', 'kln_b', 'vln_w', 'vln_b', 'W_proj', 'b_proj')}
    del _L1_attn_all

    def _L1_ffn_setup():
        import jax, jax.numpy as jnp
        import numpy as np
        DIM = 64
        HEADS = 8
        NUM_KEYS = 64
        NUM_KV = NUM_KEYS ** 2
        PK_TOPK = 16
        FINAL_TOPK = 16
        DIM_KEY = DIM // 2
        P = 2

        def _pk(x, Wq_pk, pk_keys):
            b, n, _ = x.shape
            q = (x @ Wq_pk).reshape(b, n, P, HEADS, DIM_KEY).transpose(2, 0, 1, 3, 4)
            sim = jnp.einsum('pbnhd,pkhd->pbnhk', q, pk_keys)
            scores, idx = jax.lax.top_k(sim, PK_TOPK)
            idx0 = idx[0]
            idx1 = idx[1] * NUM_KEYS
            index = (idx0[..., :, None] + idx1[..., None, :]).reshape(b, n, HEADS, PK_TOPK * PK_TOPK)
            score = (scores[0][..., :, None] + scores[1][..., None, :]).reshape(b, n, HEADS, PK_TOPK * PK_TOPK)
            final_scores, pk_idx = jax.lax.top_k(score, FINAL_TOPK)
            final_indices = jnp.take_along_axis(index, pk_idx, axis=-1)
            final_scores = jax.nn.softmax(final_scores, axis=-1)
            return (final_scores, final_indices)
        key = jax.random.key(seed)
        ks = jax.random.split(key, 7)
        b, n = (2, 256)
        std = 0.02
        x = jax.random.normal(ks[0], (b, n, DIM), dtype=jnp.float32)
        Wq_pk = jax.random.normal(ks[1], (DIM, P * HEADS * DIM_KEY), dtype=jnp.float32) * std
        pk_keys = jax.random.normal(ks[2], (P, NUM_KEYS, HEADS, DIM_KEY), dtype=jnp.float32) * std
        Wq = jax.random.normal(ks[3], (DIM, HEADS * DIM), dtype=jnp.float32) * std
        keys_table = jax.random.normal(ks[4], (NUM_KV * HEADS, DIM), dtype=jnp.float32) * std
        values_table = jax.random.normal(ks[5], (NUM_KV * HEADS, DIM), dtype=jnp.float32) * std
        Wo = jax.random.normal(ks[6], (DIM * HEADS, DIM), dtype=jnp.float32) * std
        return {'x': x, 'Wq_pk': Wq_pk, 'pk_keys': pk_keys, 'Wq': Wq, 'keys_table': keys_table, 'values_table': values_table, 'Wo': Wo}
    _L1_ffn_all = _L1_ffn_setup()
    _L1_ffn_in = {k: v for k, v in _L1_ffn_all.items() if k in ('Wq_pk', 'pk_keys', 'Wq', 'keys_table', 'values_table', 'Wo')}
    del _L1_ffn_all
    return {'x': x, 'cls_tok': cls_tok, 'L0_tok_W': _L0_tok_in['W'], 'L0_attn_W_Q': _L0_attn_in['W_Q'], 'L0_attn_W_K': _L0_attn_in['W_K'], 'L0_attn_W_V': _L0_attn_in['W_V'], 'L0_ffn_gate_w': _L0_ffn_in['gate_w'], 'L0_ffn_gate_b': _L0_ffn_in['gate_b'], 'L0_ffn_w1': _L0_ffn_in['w1'], 'L0_ffn_b1': _L0_ffn_in['b1'], 'L0_ffn_w2': _L0_ffn_in['w2'], 'L0_ffn_b2': _L0_ffn_in['b2'], 'L0_ffn_gamma': _L0_ffn_in['gamma'], 'L0_ffn_beta': _L0_ffn_in['beta'], 'L1_attn_W_qkv': _L1_attn_in['W_qkv'], 'L1_attn_b_qkv': _L1_attn_in['b_qkv'], 'L1_attn_kln_w': _L1_attn_in['kln_w'], 'L1_attn_kln_b': _L1_attn_in['kln_b'], 'L1_attn_vln_w': _L1_attn_in['vln_w'], 'L1_attn_vln_b': _L1_attn_in['vln_b'], 'L1_attn_W_proj': _L1_attn_in['W_proj'], 'L1_attn_b_proj': _L1_attn_in['b_proj'], 'L1_ffn_Wq_pk': _L1_ffn_in['Wq_pk'], 'L1_ffn_pk_keys': _L1_ffn_in['pk_keys'], 'L1_ffn_Wq': _L1_ffn_in['Wq'], 'L1_ffn_keys_table': _L1_ffn_in['keys_table'], 'L1_ffn_values_table': _L1_ffn_in['values_table'], 'L1_ffn_Wo': _L1_ffn_in['Wo']}

def reference(x, cls_tok, L0_tok_W, L0_attn_W_Q, L0_attn_W_K, L0_attn_W_V, L0_ffn_gate_w, L0_ffn_gate_b, L0_ffn_w1, L0_ffn_b1, L0_ffn_w2, L0_ffn_b2, L0_ffn_gamma, L0_ffn_beta, L1_attn_W_qkv, L1_attn_b_qkv, L1_attn_kln_w, L1_attn_kln_b, L1_attn_vln_w, L1_attn_vln_b, L1_attn_W_proj, L1_attn_b_proj, L1_ffn_Wq_pk, L1_ffn_pk_keys, L1_ffn_Wq, L1_ffn_keys_table, L1_ffn_values_table, L1_ffn_Wo):
    import jax
    import jax.numpy as jnp

    def _L0_tok_ref(x, W):
        import jax, jax.numpy as jnp
        import numpy as np
        PATCH_LEN = 16
        STRIDE = 8
        PAD = 8
        B, C, T, V = x.shape
        xp = jnp.pad(x, ((0, 0), (0, 0), (0, PAD), (0, 0)), mode='edge')
        Tp = T + PAD
        N = (Tp - PATCH_LEN) // STRIDE + 1
        idx = jnp.arange(N)[:, None] * STRIDE + jnp.arange(PATCH_LEN)[None, :]
        patches = xp[:, :, idx, :]
        patches = jnp.transpose(patches, (0, 4, 2, 3, 1))
        xf = jnp.fft.rfft(patches, axis=-2, norm='ortho')
        F = xf.shape[-2]
        x_real = xf.real.reshape(B, V, N, F * C)
        x_imag = xf.imag.reshape(B, V, N, F * C)
        x_emb = jnp.concatenate([x_real, x_imag], axis=-1)
        x_emb = x_emb @ W.T
        return x_emb.reshape(B, V * N, -1)

    def _L0_attn_ref(X, W_Q, W_K, W_V):
        import jax, jax.numpy as jnp
        import numpy as np
        GAMMA = 0.96875
        ROPE_THETA = 10000.0

        def _rope(x):
            B, S, d = x.shape
            inv_freq = 1.0 / ROPE_THETA ** (jnp.arange(0, d, 2, dtype=jnp.float32) / d)
            angles = jnp.arange(S, dtype=jnp.float32)[:, None] * inv_freq[None, :]
            cos = jnp.cos(angles).astype(x.dtype)
            sin = jnp.sin(angles).astype(x.dtype)
            xs = x.reshape(B, S, d // 2, 2)
            x0, x1 = (xs[..., 0], xs[..., 1])
            out = jnp.stack([x0 * cos - x1 * sin, x1 * cos + x0 * sin], axis=-1)
            return out.reshape(B, S, d)

        def _decay_mask(S, dtype):
            n = jnp.arange(S)[:, None]
            m = jnp.arange(S)[None, :]
            diff = n - m
            D = jnp.exp(jnp.maximum(diff, 0).astype(jnp.float32) * np.log(GAMMA))
            return jnp.where(diff >= 0, D, 0.0).astype(dtype)
        B, S, _ = X.shape
        D = _decay_mask(S, X.dtype)
        Q = _rope(X @ W_Q)
        K = _rope(X @ W_K)
        V = X @ W_V
        ret = jnp.einsum('bqd,bkd->bqk', Q, K) * D[None]
        return ret @ V

    def _L0_ffn_ref(x, gate_w, gate_b, w1, b1, w2, b2, gamma, beta):
        import jax, jax.numpy as jnp
        import numpy as np
        B, S, H, F, E, K = (8, 1024, 64, 128, 16, 2)
        EPS = 1e-05
        gate_logits = x @ gate_w + gate_b
        topk_vals, topk_idx = jax.lax.top_k(gate_logits, K)
        topk_w = jax.nn.softmax(topk_vals, axis=-1)
        h = jax.nn.relu(jnp.einsum('bsh,ehf->bsef', x, w1) + b1)
        expert_out = jnp.einsum('bsef,efh->bseh', h, w2) + b2
        sel = jnp.take_along_axis(expert_out, topk_idx[:, :, :, None], axis=2)
        moe = jnp.sum(topk_w[..., None] * sel, axis=2)
        y = x + moe
        mu = jnp.mean(y, axis=-1, keepdims=True)
        var = jnp.var(y, axis=-1, keepdims=True)
        return (y - mu) / jnp.sqrt(var + EPS) * gamma + beta

    def _L1_attn_ref(x, W_qkv, b_qkv, kln_w, kln_b, vln_w, vln_b, W_proj, b_proj):
        import jax, jax.numpy as jnp
        import numpy as np
        MIDC = 64
        HEADS = 16
        HEADC = MIDC // HEADS
        EPS = 1e-05

        def _layernorm(x, w, b):
            mean = jnp.mean(x, axis=-1, keepdims=True)
            std = jnp.std(x, axis=-1, keepdims=True, ddof=1)
            return w * (x - mean) / (std + EPS) + b
        B, HW, C = x.shape
        bias = x
        qkv = jnp.einsum('bnc,oc->bno', x, W_qkv) + b_qkv
        qkv = qkv.reshape(B, HW, HEADS, 3 * HEADC).transpose(0, 2, 1, 3)
        q, k, v = jnp.split(qkv, 3, axis=-1)
        k = _layernorm(k, kln_w, kln_b)
        v = _layernorm(v, vln_w, vln_b)
        kv = jnp.einsum('bhnd,bhne->bhde', k, v) / HW
        out = jnp.einsum('bhnd,bhde->bhne', q, kv)
        out = out.transpose(0, 2, 1, 3).reshape(B, HW, C)
        ret = out + bias
        proj = jnp.einsum('bnc,oc->bno', ret, W_proj) + b_proj
        return jax.nn.gelu(proj, approximate=False) + bias

    def _L1_ffn_ref(x, Wq_pk, pk_keys, Wq, keys_table, values_table, Wo):
        import jax, jax.numpy as jnp
        import numpy as np
        DIM = 64
        HEADS = 8
        NUM_KEYS = 64
        NUM_KV = NUM_KEYS ** 2
        PK_TOPK = 16
        FINAL_TOPK = 16
        DIM_KEY = DIM // 2
        P = 2

        def _pk(x, Wq_pk, pk_keys):
            b, n, _ = x.shape
            q = (x @ Wq_pk).reshape(b, n, P, HEADS, DIM_KEY).transpose(2, 0, 1, 3, 4)
            sim = jnp.einsum('pbnhd,pkhd->pbnhk', q, pk_keys)
            scores, idx = jax.lax.top_k(sim, PK_TOPK)
            idx0 = idx[0]
            idx1 = idx[1] * NUM_KEYS
            index = (idx0[..., :, None] + idx1[..., None, :]).reshape(b, n, HEADS, PK_TOPK * PK_TOPK)
            score = (scores[0][..., :, None] + scores[1][..., None, :]).reshape(b, n, HEADS, PK_TOPK * PK_TOPK)
            final_scores, pk_idx = jax.lax.top_k(score, FINAL_TOPK)
            final_indices = jnp.take_along_axis(index, pk_idx, axis=-1)
            final_scores = jax.nn.softmax(final_scores, axis=-1)
            return (final_scores, final_indices)
        b, n, d = x.shape
        q = (x @ Wq).reshape(b, n, HEADS, DIM) * DIM ** (-0.5)
        kv_scores, indices = _pk(x, Wq_pk, pk_keys)
        offsets = jnp.arange(HEADS, dtype=indices.dtype) * NUM_KV
        ind = indices + offsets[None, None, :, None]
        k = jnp.einsum('bnhk,bnhkd->bnhd', kv_scores, keys_table[ind])
        v = jnp.einsum('bnhk,bnhkd->bnhd', kv_scores, values_table[ind])
        sim = jnp.einsum('bihd,bjhd->bhij', q, k)
        neg = -jnp.finfo(sim.dtype).max
        causal = jnp.tril(jnp.ones((n, n), dtype=bool))
        sim = jnp.where(causal, sim, neg)
        attn = jax.nn.softmax(sim, axis=-1)
        out = jnp.einsum('bhij,bjhd->bhid', attn, v)
        out = out.transpose(0, 2, 1, 3).reshape(b, n, HEADS * DIM)
        return out @ Wo
    h = _L0_tok_ref(x, L0_tok_W)
    h = jnp.concatenate([jnp.broadcast_to(cls_tok, (h.shape[0], 1, h.shape[2])), h], axis=1)
    h = h + _L0_attn_ref(_layernorm(h, axis=-1), L0_attn_W_Q, L0_attn_W_K, L0_attn_W_V)
    h = h + _L0_ffn_ref(_layernorm(h, axis=-1), L0_ffn_gate_w, L0_ffn_gate_b, L0_ffn_w1, L0_ffn_b1, L0_ffn_w2, L0_ffn_b2, L0_ffn_gamma, L0_ffn_beta)
    h = h + _L1_attn_ref(_layernorm(h, axis=-1), L1_attn_W_qkv, L1_attn_b_qkv, L1_attn_kln_w, L1_attn_kln_b, L1_attn_vln_w, L1_attn_vln_b, L1_attn_W_proj, L1_attn_b_proj)
    h = h + _L1_ffn_ref(_layernorm(h, axis=-1), L1_ffn_Wq_pk, L1_ffn_pk_keys, L1_ffn_Wq, L1_ffn_keys_table, L1_ffn_values_table, L1_ffn_Wo)
    return h

_drawn_inputs = setup_inputs


def setup_inputs(seed=0):
    import zlib

    import numpy as np

    out = dict(_drawn_inputs(seed))
    spreads = {'L0_ffn_gate_b': (0.0, 0.1),
     'L0_ffn_b1': (0.0, 0.8),
     'L0_ffn_b2': (0.0, 0.1),
     'L0_ffn_gamma': (1.0, 0.2),
     'L0_ffn_beta': (0.0, 0.1),
     'L1_attn_b_qkv': (0.0, 0.8),
     'L1_attn_kln_w': (1.0, 0.6),
     'L1_attn_kln_b': (0.0, 0.8),
     'L1_attn_vln_w': (1.0, 0.6),
     'L1_attn_vln_b': (0.0, 0.8),
     'L1_attn_b_proj': (0.0, 0.433)}
    factors = {'L0_ffn_w1': 5.417,
     'L0_ffn_w2': 4.023,
     'L1_attn_W_qkv': 8.0,
     'L1_ffn_Wq_pk': 64.0,
     'L1_ffn_pk_keys': 60.428,
     'L1_ffn_Wq': 64.0,
     'L1_ffn_keys_table': 64.0,
     'L1_ffn_values_table': 53.717,
     'L1_ffn_Wo': 57.954}
    for name, (base, spread) in spreads.items():
        noise = np.random.default_rng([zlib.crc32(name.encode()), seed]).standard_normal(out[name].shape)
        drawn = base * np.exp(spread * noise) if base else spread * noise
        out[name] = jnp.asarray(drawn.astype(out[name].dtype))
    for name, factor in factors.items():
        out[name] = (out[name] * factor).astype(out[name].dtype)
    return out
```

```python
from contextlib import ExitStack

import numpy as np

import concourse.bass as bass
import concourse.mybir as mybir
from concourse.alu_op_type import AluOpType as ALU

F32 = mybir.dt.float32
F16 = mybir.dt.float16
BF16 = mybir.dt.bfloat16
ACT = mybir.ActivationFunctionType
AX_X = mybir.AxisListType.X

B, C_IN, T_IN, V_IN = 8, 64, 128, 64
D = 64
PATCH, STRIDE = 16, 8
NPATCH = T_IN // STRIDE
SEQ = 1 + V_IN * NPATCH
P = 114
NI = 9
PAD = NI * P
G = NI * B
HALF = 4 * P
EPS = 1e-5
NE, F = 16, 128
GAMMA = 0.96875
H = 8
NK = 64
TOPK = 16
C3 = 3 * P
NC = G // 3
SHIFT = 40.0
NEG = -1.0e30

CAND = [(0, 1, 16), (1, 1, 8), (2, 2, 5), (4, 4, 3), (8, 8, 1)]
NCAND = sum(n * m for _, n, m in CAND)


def constants():
    c = {}
    c["ident"] = np.eye(128, dtype=np.float32)
    k = np.arange(PATCH)[None, :] * np.arange(PATCH // 2 + 1)[:, None] * (2 * np.pi / PATCH)
    c["dft"] = (np.concatenate([np.cos(k), -np.sin(k)]) / np.sqrt(PATCH)).astype(np.float32)
    inv = (np.float32(1.0) / np.float32(10000.0) ** (np.arange(0, D, 2, dtype=np.float32) / np.float32(D))).astype(np.float32)
    ang = np.arange(PAD, dtype=np.float32)[:, None] * inv[None, :]
    cs = np.stack([np.cos(ang), np.sin(ang)], 1).astype(np.float32)
    c["rope"] = np.ascontiguousarray(cs.reshape(NI, P, 2 * 32))
    m, n = np.arange(P)[:, None], np.arange(P)[None, :]
    lg = np.log(GAMMA)
    c["decay"] = np.where(n >= m, np.exp(np.maximum(n - m, 0) * lg), 0.0).astype(np.float32)
    p = np.arange(P)
    c["edge"] = np.stack([np.exp((p + 1) * lg), np.exp((P - 1 - p) * lg)], 1).astype(np.float32)
    valid = np.ones((NI, P, 1), np.float32) / SEQ
    valid[NI - 1, P - 1] = 0.0
    c["valid"] = valid
    hd = np.arange(D) // 4
    c["headmask"] = (hd[:, None] == hd[None, :]).astype(np.float32)
    c["causal"] = np.stack([np.where(n > m, NEG, 0.0), np.where(n < m, NEG, 0.0)], 1).astype(np.float32)
    sel = np.zeros((2, 2, 64, 8, 4, 32), np.float16)
    for s in range(8):
        for jj in range(4):
            for ii in range(32):
                for o in range(2):
                    for part, size in enumerate((1.0, 2.0 ** -11)):
                        sel[o, o, 32 * part + ii, s, jj, ii] = size
                        sel[o, 1 - o, 32 * part + 4 * s + jj, s, jj, ii] = size
    c["sel"] = np.ascontiguousarray(sel.reshape(2, 128, 8 * 128).transpose(1, 0, 2)).reshape(128, 2 * 8 * 128)
    return c


class Chain:

    def __init__(self, eng, sem):
        self.eng, self.sem, self.n = eng, sem, 0

    def __call__(self, ins):
        self.send(ins)
        self.join()

    def send(self, ins):
        ins.then_inc(self.sem, 1)
        self.n += 1

    def join(self):
        if self.n:
            self.eng.wait_ge(self.sem, self.n)

    def restart(self):
        self.join()
        self.eng.sem_clear(self.sem)
        self.n = 0


def wait_alone(eng, sem, value, passed):
    eng.wait_ge(sem, value)
    eng.sem_inc(passed, 1)


def pool_of(ctx, nc, phase):
    def sb(name, shape, dt=F32):
        return ctx.enter_context(nc.sbuf_tensor(phase + "_sb_" + name, shape, dt))

    def ps(name, shape, dt=F32):
        return ctx.enter_context(nc.psum_tensor(phase + "_" + name, shape, dt))

    def sem(name):
        return ctx.enter_context(nc.semaphore(phase + "_" + name))

    return sb, ps, sem


def embed(nc, t, d):
    with ExitStack() as ctx:
        sb, ps, sem = pool_of(ctx, nc, "embed")
        dft = sb("dft_sb", [18, PATCH])
        wsp = sb("wsp", [18, C_IN * D])
        fold = sb("fold", [PATCH, C_IN * D])
        gw = sb("gw_sb", [128, PATCH // 2, D])
        xt = sb("xt", [128, 2, 4, 17, V_IN])
        eo = sb("eo", [128, 2, 8, D])
        psF = ps("psF", [128, 4, 512])
        psE = ps("psE", [128, 2, 512])
        s_w, s_fold, s_foldc, s_gw = sem("weights_in"), sem("fold_ps"), sem("fold_sb"), sem("gw_in")
        s_x = [sem("x_in0"), sem("x_in1")]
        s_o = [sem("out_stored0"), sem("out_stored1")]
        s_ps, s_sb, s_passed = sem("tok_ps"), sem("tok_sb"), sem("waits_passed")
        block = ctx.enter_context(nc.Block())
        xv = t["x"].rearrange("(i k) r n -> i k r n", k=2)
        h0 = d["h0"].rearrange("(i k) s o -> i k s o", k=2)

        @block.sync
        def _(sp):
            sp.dma_start(dft[:, :], t["dft"]).then_inc(s_w, 16)
            sp.dma_start(wsp[:, :], t["L0_tok_W"]).then_inc(s_w, 16)
            for b in range(B):
                sp.dma_start(d["h0"][b, 0:1, :], t["cls_tok"]).then_inc(s_w, 16)
                sp.dma_start(d["h0"][b, SEQ:PAD, :], t["cls_tok"]).then_inc(s_w, 16)
            sp.wait_ge(s_foldc, 8)
            sp.dma_start(d["gw"], fold[:, :]).then_inc(s_gw, 16)
            sp.wait_ge(s_gw, 16)
            for two in range(2):
                sp.dma_start(gw[64 * two:64 * two + 64, :, :],
                             d["gw"].rearrange("(q two) (c o) -> two c q o", two=2, c=C_IN)[two]
                             ).then_inc(s_gw, 16)
            sp.wait_ge(s_w, 16 * 18)
            with sp.Fori(0, B // 2) as i:
                ready = [sp.snap(i * 4 + 1), sp.snap(i * 4 + 3)]
                for k in range(2):
                    wait_alone(sp, s_ps, ready[k], s_passed)
                    sp.dma_start(xt[:, k, :, :, :], xv[i, k]).then_inc(s_x[k], 16)

        @block.tensor
        def _(pe):
            pe.wait_ge(s_w, 16 * 18)
            for n in range(8):
                if n >= 4:
                    pe.wait_ge(s_foldc, n - 3)
                nc.tensor.matmul(psF[0:PATCH, n % 4, :], dft[:, :], wsp[:, n * 512:(n + 1) * 512],
                                 start=True, stop=True).then_inc(s_fold, 1)
            pe.wait_ge(s_gw, 48)
            pe.sem_inc(s_ps, 3)
            with pe.Fori(0, B // 2) as i:
                for k in range(2):
                    pe.wait_ge(s_x[k], (i + 1) * 16)
                    for half in range(2):
                        pe.wait_ge(s_sb, i * 4 + (2 * k + half + 1))
                        for vt in range(4):
                            n0 = 2 * (4 * half + vt)
                            for q in range(PATCH // 2):
                                xq = xt[:, k, q % 4, n0 + q // 4:n0 + q // 4 + 2, :].rearrange("p m v -> p (m v)")
                                mm = nc.tensor.matmul(psE[:, half, vt * D:(vt + 1) * D], xq, gw[:, q, :],
                                                      start=(q == 0), stop=(q == PATCH // 2 - 1))
                        mm.then_inc(s_ps, 1)

        @block.vector
        def _(dve):
            for n in range(8):
                dve.wait_ge(s_fold, n + 1)
                nc.vector.tensor_copy(fold[:, n * 512:(n + 1) * 512], psF[0:PATCH, n % 4, :]).then_inc(s_foldc, 1)
            dve.sem_inc(s_sb, 2)
            with dve.Fori(0, B // 2) as i:
                for k in range(2):
                    for half in range(2):
                        dve.wait_ge(s_o[k], (i + 1) * 32)
                        dve.wait_ge(s_ps, i * 4 + (2 * k + half + 4))
                        nc.vector.tensor_copy(eo[:, k, 4 * half:4 * half + 4, :],
                                              psE[:, half, 0:4 * D]).then_inc(s_sb, 1)

        @block.scalar
        def _(act):
            for k in range(2):
                act.sem_inc(s_o[k], 32)
            with act.Fori(0, B // 2) as i:
                for k in range(2):
                    act.wait_ge(s_sb, i * 4 + (2 * k + 4))
                    for n2 in range(2):
                        act.dma_start(h0[i, k, 1:SEQ, :].rearrange("(v vt two) o -> two v vt o", vt=8, two=2)[n2],
                                      eo[64 * n2:64 * n2 + 64, k, :, :]).then_inc(s_o[k], 16)
            for k in range(2):
                act.wait_ge(s_o[k], 32 * (B // 2 + 1))


def lay_out_x(x):
    x = np.concatenate([x] + [x[:, :, -1:, :]] * STRIDE, axis=2)
    x = x.reshape(B, C_IN, 17, 4, 2, V_IN).transpose(0, 4, 1, 3, 2, 5)
    return np.ascontiguousarray(x).reshape(B, 2 * C_IN, 4 * 17 * V_IN)


def layer0_and_kv(nc, t, d, kvs):
    with ExitStack() as ctx:
        sb, ps, sem = pool_of(ctx, nc, "layer0")
        ident = sb("ident", [128, 128])
        decay = sb("decay", [P, P])
        edge = sb("edge", [P, 2])
        wqk, wv = sb("wqk", [D, 2 * D]), sb("wv", [D, D])
        gate_w, gate_b = sb("gate_w", [D, NE]), sb("gate_b", [P, NE])
        w1, b1 = sb("w1", [D, NE, F]), sb("b1", [F, NE])
        w2, b2 = sb("w2", [F, NE, D]), sb("b2", [NE, D])
        ln_g, ln_b = sb("ln_g", [P, D]), sb("ln_b", [P, D])
        wq3, wkv3 = sb("wq3", [D, D]), sb("wkv3", [D, 2 * D])
        bq3, bkv3 = sb("bq3", [D, 1]), sb("bkv3", [P, 2 * D])
        hln_w, hln_b = sb("hln_w", [P, 2 * D]), sb("hln_b", [P, 2 * D])
        rope, valid = sb("rope", [P, 2, 32]), sb("valid", [P, 1])
        hb = sb("hb", [P, B, D])
        xn = sb("xn", [P, B, D])
        acc = sb("acc", [P, B, D])
        sq = sb("sq", [P, B, D])
        st = sb("st", [P, 3, B])
        xT = sb("xT", [D, 2, HALF])
        xTb = xT[:, :, :].rearrange("d u (b p) -> d (u b) p", p=P)
        vs = sb("vs", [P, B, D])
        ra = sb("ra", [P, 2 * B, 2, 32])
        rb = sb("rb", [P, 2 * B, 2, 32])
        qk = sb("qk", [P, B, 2, D])
        ks = sb("ks", [P, B, D])
        qkT = sb("qkT", [D, 2, 2, HALF])
        aT = sb("aT", [P, 2, HALF])
        state = sb("state", [D, B, D])
        lg, ex = sb("lg", [P, B, NE]), sb("ex", [P, B, NE])
        rep, gates = sb("rep", [P, B, NE]), sb("gates", [P, B, NE])
        m8, mt = sb("m8", [P, B, 8]), sb("mt", [P, B, 8])
        gz = sb("gz", [P, B])
        gT = sb("gT", [NE, 2, HALF])
        hid = sb("hid", [F, 2, 2, HALF])
        q3T = sb("q3T", [D, 2, HALF])
        kv = ra[:, :, :, :].rearrange("p (b w) x e -> p b (w x e)", b=B)
        kq = rb[:, :, :, :].rearrange("p (b w) x e -> p b (w x e)", b=B)
        gs = sb("gs", [P, 2, B * 2 * D // 4])
        psX, psY, psQ = ps("psX", [128, 2, 512]), ps("psY", [128, 2, 512]), ps("psQ", [128, 2, 512])
        psV = ps("psV", [128, 512])

        s_c, s_load, s_store, s_passed = sem("consts_in"), sem("tile_in"), sem("tile_stored"), sem("waits_passed")
        s_dve = sem("dve_chain")
        s_pe = sem("pe_products")
        s_xn, s_x2, s_x3 = sem("xn"), sem("x2"), sem("x3")
        s_xT, s_x2T, s_x3T = sem("xT"), sem("x2T"), sem("x3T")
        s_qk, s_v, s_qkT, s_aT, s_inter = sem("qk"), sem("v"), sem("qkT"), sem("aT"), sem("inter_used")
        s_lgm, s_ex, s_gates, s_gT, s_acc0 = sem("lgm"), sem("ex"), sem("gates"), sem("gT"), sem("acc0")
        s_hid, s_h1, s_eo, s_ed = sem("hid"), sem("hid_ps"), sem("expert_ps"), sem("expert_added")
        s_q3, s_kv, s_kvn, s_pe3 = sem("q3"), sem("kv_summed"), sem("kv_normed"), sem("pe_kv")
        s_var, s_std = sem("var"), sem("std")
        block = ctx.enter_context(nc.Block())
        NPE = 9

        @block.sync
        def _(sp):
            loads = [(ident, t["ident"]), (decay, t["decay"]), (edge, t["edge"]), (wqk, t["wqk"]), (wv, t["wv"]),
                     (gate_w, t["gate_w"]), (gate_b, t["gate_b"].to_broadcast([P, NE])), (b1, t["b1"]),
                     (b2, t["b2"]), (ln_g, t["ln_g"].to_broadcast([P, D])), (ln_b, t["ln_b"].to_broadcast([P, D])),
                     (wq3, t["wq3"]), (wkv3, t["wkv3"]), (bq3, t["bq3"]), (bkv3, t["bkv3"].to_broadcast([P, 2 * D])),
                     (hln_w, t["hln_w"].to_broadcast([P, 2 * D])), (hln_b, t["hln_b"].to_broadcast([P, 2 * D]))]
            for dst, src in loads:
                sp.dma_start(dst[:, :], src).then_inc(s_c, 16)
            sp.dma_start(w1[:, :, :], t["w1"]).then_inc(s_c, 16)
            sp.dma_start(w2[:, :, :], t["w2"]).then_inc(s_c, 16)
            with sp.Fori(0, NI) as i:
                nxt, stored = sp.snap(i + 1), sp.snap(i * 64 + 64)
                h_in = d["h0"].rearrange("b (i p) o -> i p b o", p=P)[i]
                sp.dma_start(hb[:, :, :], h_in).then_inc(s_load, 16)
                sp.dma_start(rope[:, :, :], t["rope"][i]).then_inc(s_load, 16)
                sp.dma_start(valid[:, :], t["valid"][i]).then_inc(s_load, 16)
                wait_alone(sp, s_kv, nxt, s_passed)
                wait_alone(sp, s_q3, nxt, s_passed)
                sp.dma_start(d["h1"][i], hb[:, :, :]).then_inc(s_store, 16)
                sp.dma_start(d["x3"][i], xn[:, :, :]).then_inc(s_store, 16)
                sp.dma_start(d["x3T"][i], xT[:, :, :]).then_inc(s_store, 16)
                sp.dma_start(d["q3T"][i], q3T[:, :, :]).then_inc(s_store, 16)
                wait_alone(sp, s_store, stored, s_passed)

        @block.tensor
        def _(pe):
            def to_T(src, into, n=B):
                for b in range(n):
                    mm = pe.transpose(into[0:src.shape[2], b // 4, (b % 4) * P:(b % 4 + 1) * P], src[:, b, :], ident[0:P, 0:P])
                return mm

            pe.wait_ge(s_c, 16 * 19)
            with pe.Fori(0, NI) as i:
                nxt = i + 1
                wait_alone(pe, s_xn, nxt, s_passed)
                to_T(xn, psX).then_inc(s_pe, 1)
                pe.wait_ge(s_xT, nxt)
                for b in range(B):
                    pe.matmul(psQ[0:P, b // 4, (b % 4) * 128:(b % 4 + 1) * 128], xTb[:, b, :], wqk[:, :], start=True, stop=True)
                    mm = pe.matmul(psV[0:P, b * D:(b + 1) * D], xTb[:, b, :], wv[:, :], start=True, stop=True)
                mm.then_inc(s_pe, 1)
                wait_alone(pe, s_qk, nxt, s_passed)
                to_T(qk[:, :, 0, :], psX)
                to_T(qk[:, :, 1, :], psY).then_inc(s_pe, 1)
                pe.wait_ge(s_qkT, nxt)
                pe.wait_ge(s_v, nxt)
                for b in range(B):
                    c0 = slice((b % 4) * P, (b % 4 + 1) * P)
                    qb, kb = qkT[:, 0, b // 4, c0], qkT[:, 1, b // 4, c0]
                    pe.matmul(psX[0:P, b // 4, c0], kb, qb, start=True, stop=True)
                    pe.matmul(psV[0:P, b * D:(b + 1) * D], qb, state[:, b, :], start=True, stop=True)
                    mm = pe.matmul(psQ[0:D, 0, b * D:(b + 1) * D], ks[:, b, :], vs[:, b, :], start=True, stop=True)
                mm.then_inc(s_pe, 1)
                pe.wait_ge(s_aT, nxt)
                for b in range(B):
                    mm = pe.matmul(psQ[0:P, 1, b * D:(b + 1) * D], aT[:, b // 4, (b % 4) * P:(b % 4 + 1) * P],
                                   vs[:, b, :], start=True, stop=True)
                mm.then_inc(s_pe, 1)
                wait_alone(pe, s_x2, nxt, s_passed)
                to_T(xn, psX).then_inc(s_pe, 1)
                pe.wait_ge(s_x2T, nxt)
                for b in range(B):
                    mm = pe.matmul(psV[0:P, b * NE:(b + 1) * NE], xTb[:, b, :], gate_w[:, :], start=True, stop=True)
                mm.then_inc(s_pe, 1)
                wait_alone(pe, s_gates, nxt, s_passed)
                to_T(gates, psY).then_inc(s_pe, 1)
                pe.wait_ge(s_gT, nxt)
                for b in range(B):
                    mm = pe.matmul(psV[0:P, b * D:(b + 1) * D], gT[:, b // 4, (b % 4) * P:(b % 4 + 1) * P], b2[:, :],
                                   start=True, stop=True)
                mm.then_inc(s_pe, 1)
                for e in range(NE + 1):
                    if e < NE:
                        bank = (psX, psY)[e % 2]
                        if e >= 2:
                            pe.wait_ge(s_hid, i * NE + (e - 1))
                        for u in range(2):
                            mm = pe.matmul(bank[:, u, 0:HALF], w1[:, e, :], xT[:, u, :], start=True, stop=True)
                        mm.then_inc(s_h1, 1)
                    if e >= 1:
                        k = e - 1
                        pe.wait_ge(s_hid, i * NE + (k + 1))
                        if k >= 2:
                            pe.wait_ge(s_ed, i * NE + (k - 1))
                        for b in range(B):
                            mm = pe.matmul(psQ[0:P, k % 2, b * D:(b + 1) * D],
                                           hid[:, k % 2, b // 4, (b % 4) * P:(b % 4 + 1) * P], w2[:, k, :],
                                           start=True, stop=True)
                        mm.then_inc(s_eo, 1)
                wait_alone(pe, s_x3, nxt, s_passed)
                to_T(xn, psX).then_inc(s_pe3, 1)
                pe.wait_ge(s_x3T, nxt)
                for b in range(B):
                    pe.matmul(psQ[0:P, b // 4, (b % 4) * 128:(b % 4 + 1) * 128], xTb[:, b, :], wkv3[:, :], start=True, stop=True)
                for u in range(2):
                    mm = pe.matmul(psY[0:D, u, 0:HALF], wq3[:, :], xT[:, u, :], start=True, stop=True)
                mm.then_inc(s_pe3, 1)
                pe.wait_ge(s_kvn, nxt)
                for b in range(B):
                    mm = pe.matmul(psV[0:D, b * D:(b + 1) * D], kv[:, b, 0:D], kv[:, b, D:2 * D], start=True, stop=True)
                mm.then_inc(s_pe3, 1)

        @block.scalar
        def _(act):
            act.wait_ge(s_c, 16 * 19)
            with act.Fori(0, NI) as i:
                nxt = i + 1

                def products(n):
                    act.wait_ge(s_pe, i * NPE + n)

                def copy_T(src, dst, s, rows=D):
                    for u in range(2):
                        ins = act.copy(dst[0:rows, u, :], src[0:rows, u, 0:HALF])
                    ins.then_inc(s, 1)

                def root(n, x=st[:, 1, :], out=st[:, 2, :]):
                    act.wait_ge(s_var, i * 5 + n)
                    act.activation(out, x, ACT.Sqrt).then_inc(s_std, 1)

                root(1)
                products(1)
                copy_T(psX, xT, s_xT)
                products(2)
                act.copy(vs[:, :, :], psV[0:P, :]).then_inc(s_v, 1)
                products(3)
                for w in range(2):
                    for u in range(2):
                        ins = act.copy(qkT[:, w, u, :], (psX, psY)[w][0:D, u, 0:HALF])
                ins.then_inc(s_qkT, 1)
                root(2)
                products(6)
                copy_T(psX, xT, s_x2T)
                act.wait_ge(s_lgm, nxt)
                act.activation(ex[:, :, :], lg[:, :, :], ACT.Exp).then_inc(s_ex, 1)
                products(8)
                copy_T(psY, gT, s_gT, NE)
                for e in range(NE):
                    act.wait_ge(s_h1, i * NE + (e + 1))
                    if e >= 2:
                        act.wait_ge(s_eo, i * NE + (e - 1))
                    for u in range(2):
                        ins = act.activation(hid[:, e % 2, u, :], (psX, psY)[e % 2][:, u, 0:HALF], ACT.Relu, bias=b1[:, e:e + 1])
                    ins.then_inc(s_hid, 1)
                root(3)
                root(4)
                act.wait_ge(s_pe3, i * 3 + 1)
                copy_T(psX, xT, s_x3T)
                act.wait_ge(s_pe3, i * 3 + 2)
                for u in range(2):
                    ins = act.activation(q3T[:, u, :], psY[0:D, u, 0:HALF], ACT.Identity, bias=bq3[:, 0:1])
                ins.then_inc(s_q3, 1)
                root(5, gs[:, 0, :], gs[:, 1, :])

        @block.vector
        def _(dve):
            c = Chain(dve, s_dve)
            v = nc.vector
            c.send(v.memset(state[:, :, :], 0.0))
            c.send(v.memset(kvs[:, :, :], 0.0))
            c.send(v.memset(mt[:, :, :], 3.0e38))
            c.restart()
            dve.wait_ge(s_c, 16 * 19)
            with dve.Fori(0, NI) as i:
                nxt = i + 1

                def products(n):
                    dve.wait_ge(s_pe, i * NPE + n)

                def norm(x, out, n, done=None):
                    mean, var, std = st[:, 0, :], st[:, 1, :], st[:, 2, :]
                    full = [P, B, D]
                    c(v.tensor_reduce(mean, x, AX_X, ALU.add))
                    c(v.tensor_scalar(mean, mean, 1.0 / D, None, ALU.mult))
                    c(v.tensor_tensor(out, x, mean.unsqueeze(2).to_broadcast(full), ALU.subtract))
                    c(v.tensor_tensor(sq[:, :, :], out, out, ALU.mult))
                    c(v.tensor_reduce(var, sq[:, :, :], AX_X, ALU.add))
                    v.tensor_scalar(var, var, 1.0 / D, EPS, ALU.mult, ALU.add).then_inc(s_var, 1)
                    dve.wait_ge(s_std, i * 5 + n)
                    c(v.reciprocal(std, std))
                    ins = v.tensor_tensor(out, out, std.unsqueeze(2).to_broadcast(full), ALU.mult)
                    if done is None:
                        c(ins)
                    else:
                        ins.then_inc(done, 1)
                        dve.wait_ge(done, nxt)

                dve.wait_ge(s_load, i * 48 + 48)
                norm(hb[:, :, :], xn[:, :, :], 1, s_xn)
                products(2)
                for u in range(2):
                    src = psQ[0:P, u, :].rearrange("p (a e) -> p a e", e=32)
                    c.send(v.tensor_tensor(ra[:, 8 * u:8 * u + 8, :, :].rearrange("p a w e -> p (a w) e"), src,
                                           rope[:, 0, :].unsqueeze(1).to_broadcast([P, 16, 32]), ALU.mult))
                    c.send(v.tensor_tensor(rb[:, 8 * u:8 * u + 8, :, :].rearrange("p a w e -> p (a w) e"), src,
                                           rope[:, 1, :].unsqueeze(1).to_broadcast([P, 16, 32]), ALU.mult))
                c.join()
                qk4 = qk[:, :, :, :].rearrange("p b w (x e) -> p (b w) x e", x=2)
                c.send(v.tensor_tensor(qk4[:, :, 0, :], ra[:, :, 0, :], rb[:, :, 1, :], ALU.subtract))
                c(v.tensor_tensor(qk4[:, :, 1, :], ra[:, :, 1, :], rb[:, :, 0, :], ALU.add))
                v.tensor_scalar(ks[:, :, :], qk[:, :, 1, :], edge[:, 1:2], None, ALU.mult).then_inc(s_qk, 1)
                products(4)
                for u in range(2):
                    ins = v.tensor_tensor(aT[:, u, :].rearrange("p (b n) -> p b n", b=4),
                                          psX[0:P, u, 0:HALF].rearrange("p (b n) -> p b n", b=4),
                                          decay[:, :].unsqueeze(1).to_broadcast([P, 4, P]), ALU.mult)
                ins.then_inc(s_aT, 1)
                flat = "p b o -> p (b o)"
                c.send(v.scalar_tensor_tensor(hb[:, :, :].rearrange(flat), psV[0:P, :], edge[:, 0:1],
                                              hb[:, :, :].rearrange(flat), ALU.mult, ALU.add))
                c(v.scalar_tensor_tensor(state[:, :, :].rearrange(flat), state[:, :, :].rearrange(flat), float(GAMMA ** P),
                                         psQ[0:D, 0, :], ALU.mult, ALU.add))
                products(5)
                c(v.tensor_tensor(hb[:, :, :].rearrange(flat), hb[:, :, :].rearrange(flat), psQ[0:P, 1, :], ALU.add))
                norm(hb[:, :, :], xn[:, :, :], 2, s_x2)
                products(7)
                full = [P, B, NE]
                c(v.tensor_tensor(lg[:, :, :], psV[0:P, 0:B * NE].rearrange("p (b e) -> p b e", e=NE),
                                  gate_b[:, :].unsqueeze(1).to_broadcast(full), ALU.add))
                for b in range(B):
                    c.send(v.max(m8[:, b, :], lg[:, b, :]))
                c.join()
                c(v.tensor_copy(mt[:, :, 0:2], m8[:, :, 0:2]))
                for b in range(B):
                    c.send(v.match_replace(rep[:, b, :], mt[:, b, :], lg[:, b, :], -3.0e38))
                c.join()
                c(v.tensor_tensor(rep[:, :, :], rep[:, :, :], lg[:, :, :], ALU.not_equal))
                v.tensor_tensor(lg[:, :, :], lg[:, :, :], m8[:, :, 0:1].to_broadcast(full), ALU.subtract).then_inc(s_lgm, 1)
                dve.wait_ge(s_ex, nxt)
                c(v.tensor_tensor(gates[:, :, :], ex[:, :, :], rep[:, :, :], ALU.mult))
                c(v.tensor_reduce(gz[:, :], gates[:, :, :], AX_X, ALU.add))
                c(v.reciprocal(gz[:, :], gz[:, :]))
                v.tensor_tensor(gates[:, :, :], gates[:, :, :], gz[:, :].unsqueeze(2).to_broadcast(full), ALU.mult).then_inc(s_gates, 1)
                products(9)
                c(v.tensor_tensor(acc[:, :, :].rearrange(flat), xn[:, :, :].rearrange(flat), psV[0:P, :], ALU.add))
                for e in range(NE):
                    dve.wait_ge(s_eo, i * NE + (e + 1))
                    v.tensor_tensor(sq[:, :, :], psQ[0:P, e % 2, :].rearrange("p (b o) -> p b o", b=B),
                                    gates[:, :, e:e + 1].to_broadcast([P, B, D]), ALU.mult).then_inc(s_ed, 1)
                    dve.wait_ge(s_ed, i * NE + (e + 1))
                    c(v.tensor_tensor(acc[:, :, :], acc[:, :, :], sq[:, :, :], ALU.add))
                norm(acc[:, :, :], acc[:, :, :], 3)
                c(v.tensor_tensor(acc[:, :, :], acc[:, :, :], ln_g[:, :].unsqueeze(1).to_broadcast([P, B, D]), ALU.mult))
                c(v.tensor_tensor(acc[:, :, :], acc[:, :, :], ln_b[:, :].unsqueeze(1).to_broadcast([P, B, D]), ALU.add))
                c(v.tensor_tensor(hb[:, :, :], hb[:, :, :], acc[:, :, :], ALU.add))
                norm(hb[:, :, :], xn[:, :, :], 4, s_x3)
                dve.wait_ge(s_pe3, i * 3 + 2)
                kvf = kv[:, :, :].rearrange("p b n -> p (b n)")
                kvg = kv[:, :, :].rearrange("p b (g e) -> p (b g) e", e=4)
                kqg = kq[:, :, :].rearrange("p b (g e) -> p (b g) e", e=4)
                NG = B * 2 * D // 4
                c(v.tensor_tensor(kv[:, :, :], psQ[0:P, :, :].rearrange("p u (b n) -> p (u b) n", b=4),
                                  bkv3[:, :].unsqueeze(1).to_broadcast([P, B, 2 * D]), ALU.add))
                c(v.tensor_reduce(gs[:, 0, :], kvg, AX_X, ALU.add))
                c(v.tensor_scalar(gs[:, 0, :], gs[:, 0, :], 0.25, None, ALU.mult))
                c(v.tensor_tensor(kvg, kvg, gs[:, 0, :].unsqueeze(2).to_broadcast([P, NG, 4]), ALU.subtract))
                c(v.tensor_tensor(kqg, kvg, kvg, ALU.mult))
                c(v.tensor_reduce(gs[:, 0, :], kqg, AX_X, ALU.add))
                v.tensor_scalar(gs[:, 0, :], gs[:, 0, :], 1.0 / 3.0, None, ALU.mult).then_inc(s_var, 1)
                dve.wait_ge(s_std, i * 5 + 5)
                c(v.tensor_scalar(gs[:, 1, :], gs[:, 1, :], EPS, None, ALU.add))
                c(v.reciprocal(gs[:, 1, :], gs[:, 1, :]))
                c(v.tensor_tensor(kvg, kvg, gs[:, 1, :].unsqueeze(2).to_broadcast([P, NG, 4]), ALU.mult))
                c(v.tensor_tensor(kv[:, :, :], kv[:, :, :], hln_w[:, :].unsqueeze(1).to_broadcast([P, B, 2 * D]), ALU.mult))
                c(v.tensor_tensor(kv[:, :, :], kv[:, :, :], hln_b[:, :].unsqueeze(1).to_broadcast([P, B, 2 * D]), ALU.add))
                v.tensor_scalar(kv[:, :, 0:D], kv[:, :, 0:D], valid[:, 0:1], None, ALU.mult).then_inc(s_kvn, 1)
                dve.wait_ge(s_pe3, i * 3 + 3)
                v.tensor_tensor(kvs[:, :, :].rearrange(flat), kvs[:, :, :].rearrange(flat), psV[0:D, :], ALU.add).then_inc(s_kv, 1)
                wait_alone(dve, s_kv, nxt, s_passed)
                c.restart()


def linear_attention(nc, t, d, kvs):
    with ExitStack() as ctx:
        sb, ps, sem = pool_of(ctx, nc, "linear")
        ident, headmask = sb("ident", [128, 128]), sb("headmask", [D, D])
        wp, bp = sb("wp", [D, D]), sb("bp", [P, D])
        hb, x3 = sb("hb", [P, B, D]), sb("x3", [P, B, D])
        x3T, q3T = sb("x3T", [D, 2, HALF]), sb("q3T", [D, 2, HALF])
        pb, ge, xn, sq = sb("pb", [P, B, D]), sb("ge", [P, B, D]), sb("xn", [P, B, D]), sb("sq", [P, B, D])
        st = sb("st", [P, 3, B])
        xT = sb("xT", [D, 2, HALF])
        psX, psV = ps("psX", [128, 2, 512]), ps("psV", [128, 512])
        s_c, s_load, s_store, s_passed = sem("consts_in"), sem("tile_in"), sem("tile_stored"), sem("waits_passed")
        s_dve, s_kvm, s_out, s_ret = sem("dve_chain"), sem("kv_masked"), sem("out_ps"), sem("ret")
        s_proj, s_pb, s_ge, s_var, s_std = sem("proj_ps"), sem("proj_sb"), sem("gelu"), sem("var"), sem("std")
        s_xn, s_xTp, s_xT = sem("xn"), sem("xT_ps"), sem("xT")
        block = ctx.enter_context(nc.Block())

        @block.sync
        def _(sp):
            for dst, src in ((ident, t["ident"]), (headmask, t["headmask"]), (wp, t["wp3"]),
                             (bp, t["bp3"].to_broadcast([P, D]))):
                sp.dma_start(dst[:, :], src).then_inc(s_c, 16)
            with sp.Fori(0, NI) as i:
                sp.dma_start(hb[:, :, :], d["h1"][i]).then_inc(s_load, 16)
                sp.dma_start(x3[:, :, :], d["x3"][i]).then_inc(s_load, 16)
                sp.dma_start(x3T[:, :, :], d["x3T"][i]).then_inc(s_load, 16)
                sp.dma_start(q3T[:, :, :], d["q3T"][i]).then_inc(s_load, 16)
                wait_alone(sp, s_xT, i + 1, s_passed)
                sp.dma_start(d["h2"][i], hb[:, :, :]).then_inc(s_store, 16)
                sp.dma_start(d["x4T"][:, 0:G * P].rearrange("o (i u n) -> i o u n", i=NI, u=2)[i], xT[:, :, :]).then_inc(s_store, 16)
                wait_alone(sp, s_store, i * 32 + 32, s_passed)
            sp.dma_start(d["x4T"][:, G * P:G * P + C3], xT[:, 0, 0:C3]).then_inc(s_store, 16)
            sp.wait_ge(s_store, NI * 32 + 16)

        @block.tensor
        def _(pe):
            pe.wait_ge(s_c, 64)
            pe.wait_ge(s_kvm, 1)
            with pe.Fori(0, NI) as i:
                nxt = i + 1
                wait_alone(pe, s_load, i * 64 + 64, s_passed)
                for b in range(B):
                    cols = slice((b % 4) * P, (b % 4 + 1) * P)
                    mm = pe.matmul(psX[0:D, b // 4, cols], kvs[:, b, :], q3T[:, b // 4, cols], start=True, stop=True)
                mm.then_inc(s_out, 1)
                pe.wait_ge(s_ret, nxt)
                for b in range(B):
                    mm = pe.matmul(psV[0:P, b * D:(b + 1) * D], x3T[:, b // 4, (b % 4) * P:(b % 4 + 1) * P], wp[:, :],
                                   start=True, stop=True)
                mm.then_inc(s_proj, 1)
                wait_alone(pe, s_xn, nxt, s_passed)
                for b in range(B):
                    mm = pe.transpose(psX[0:D, b // 4, (b % 4) * P:(b % 4 + 1) * P], xn[:, b, :], ident[0:P, 0:P])
                mm.then_inc(s_xTp, 1)

        @block.scalar
        def _(act):
            with act.Fori(0, NI) as i:
                nxt = i + 1
                act.wait_ge(s_pb, nxt)
                act.activation(ge[:, :, :], pb[:, :, :], ACT.Gelu).then_inc(s_ge, 1)
                act.wait_ge(s_var, nxt)
                act.activation(st[:, 2, :], st[:, 1, :], ACT.Sqrt).then_inc(s_std, 1)
                act.wait_ge(s_xTp, nxt)
                for u in range(2):
                    ins = act.copy(xT[:, u, :], psX[0:D, u, 0:HALF])
                ins.then_inc(s_xT, 1)

        @block.vector
        def _(dve):
            c = Chain(dve, s_dve)
            v = nc.vector
            full = [P, B, D]
            dve.wait_ge(s_c, 64)
            v.tensor_tensor(kvs[:, :, :], kvs[:, :, :], headmask[:, :].unsqueeze(1).to_broadcast([D, B, D]),
                            ALU.mult).then_inc(s_kvm, 1)
            with dve.Fori(0, NI) as i:
                nxt = i + 1
                dve.wait_ge(s_load, i * 64 + 64)
                dve.wait_ge(s_out, nxt)
                for u in range(2):
                    ins = v.tensor_tensor(x3T[:, u, :], x3T[:, u, :], psX[0:D, u, 0:HALF], ALU.add)
                ins.then_inc(s_ret, 1)
                c(v.tensor_tensor(hb[:, :, :], hb[:, :, :], x3[:, :, :], ALU.add))
                dve.wait_ge(s_proj, nxt)
                v.tensor_tensor(pb[:, :, :], psV[0:P, :].rearrange("p (b o) -> p b o", b=B),
                                bp[:, :].unsqueeze(1).to_broadcast(full), ALU.add).then_inc(s_pb, 1)
                dve.wait_ge(s_ge, nxt)
                c(v.tensor_tensor(hb[:, :, :], hb[:, :, :], ge[:, :, :], ALU.add))
                mean, var, std = st[:, 0, :], st[:, 1, :], st[:, 2, :]
                c(v.tensor_reduce(mean, hb[:, :, :], AX_X, ALU.add))
                c(v.tensor_scalar(mean, mean, 1.0 / D, None, ALU.mult))
                c(v.tensor_tensor(xn[:, :, :], hb[:, :, :], mean.unsqueeze(2).to_broadcast(full), ALU.subtract))
                c(v.tensor_tensor(sq[:, :, :], xn[:, :, :], xn[:, :, :], ALU.mult))
                c(v.tensor_reduce(var, sq[:, :, :], AX_X, ALU.add))
                v.tensor_scalar(var, var, 1.0 / D, EPS, ALU.mult, ALU.add).then_inc(s_var, 1)
                dve.wait_ge(s_std, nxt)
                c(v.reciprocal(std, std))
                v.tensor_tensor(xn[:, :, :], xn[:, :, :], std.unsqueeze(2).to_broadcast(full), ALU.mult).then_inc(s_xn, 1)
                c.restart()


KT = 32
LA = 4
UNITS_BEFORE = 16
UNITS = 32


FREE_AT = (2, 17, 22, 27)


def units_at(h, kt):
    if h >= 1 and kt == 7:
        return [("kv", h - 1)]
    if h >= 1 and kt == 12:
        return [("keysT", h - 1)]
    if kt not in FREE_AT:
        return []
    k = FREE_AT.index(kt)
    if h == 1:
        return [("query", k)]
    g = h // 6
    n = 4 * (h - (2, 6)[g]) + k
    if h in (2, 3, 6, 7) and n < 6:
        return [("score", n // 2, 2 * (n % 2) + g)]
    return []


FIRST_UNITS = [("query", k) for k in range(4)] + [("score", t, 2 * p + g) for g in range(2) for t in range(3) for p in range(2)]
LAST_UNITS = [("kv", H - 1), ("keysT", H - 1)]
STACK_AT = {4: 0, 9: 1, 14: 2}
ACT_BEHIND, DVE_BEHIND = 4, 3
PIECES = {1: "max0", 2: "max1", 4: "drop0", 5: "drop1", 7: "next0", 8: "next1", 10: "shift",
          12: "sums", 14: "smax", 15: "sdrop", 16: "snext", 18: "bound", 20: "parts", 27: "low", 29: "scale"}


def memory(nc, t, d, tab, s_tab):
    with ExitStack() as ctx:
        sb, ps, sem = pool_of(ctx, nc, "memory")
        ident, ident16 = sb("ident", [128, 128]), sb("ident16", [128, 128], F16)
        wqpk, pkeys = sb("wqpk", [D, 4, 128]), sb("pkeys", [128, 4, 4, NK])
        sel = sb("sel", [128, 2, 8, 128], F16)
        xT = sb("xT", [D, C3])
        qpk = sb("qpk", [128, 4, C3])
        sc = sb("sc", [P, 3, 2, H, NK])
        t16, tr = sb("t16", [P, 3, 2, TOPK]), sb("tr", [P, 3, 2, TOPK])
        tmp = sb("tmp", [P, 3, 2, NK])
        cand, ctmp = sb("cand", [P, 3, NCAND]), sb("ctmp", [P, 3, NCAND])
        c16, e16 = sb("c16", [P, 3, TOPK]), sb("e16", [P, 3, TOPK])
        thr = sb("thr", [P, 3, 3])
        rz = sb("rz", [P, 3])
        ab, lo32 = sb("ab", [P, 2, 3, NK]), sb("lo32", [P, 2, 3, NK])
        stk = sb("stk", [P, 2, 3, 5, 2, 32], F16)
        stack = sb("stack", [128, 2, 4, C3], F16)
        scale = sb("scale", [P, 4, 3])
        ew, ww = sb("ew", [128, 4, C3]), sb("ww", [128, 4, C3])
        kvT = sb("kvT", [128, C3])
        kvo = sb("kvo", [P, 2, 3, 2 * D])
        kT = sb("kT", [D, 2, C3])
        psS = ps("psS", [128, 4, 512])
        psKV = ps("psKV", [128, 2, 512])
        psT = ps("psT", [128, 4, 2, P], F16)
        psM = ps("psM", [128, 512])

        s_c, s_x, s_passed, s_id = sem("consts_in"), sem("chunk_in"), sem("waits_passed"), sem("ident16")
        s_sum, s_exp, s_weight = sem("sums"), sem("exps"), sem("weights")
        s_acc, s_kvT = sem("head_product"), sem("head_product_sb")
        s_unit, s_unit_used = sem("unit"), sem("unit_used")
        s_T, s_T_used = sem("stack_ps"), sem("stack_sb")
        s_sel_chain = sem("selection_chain")
        s_bound, s_ex, s_parts, s_hi, s_lo, s_stk = sem("bound"), sem("ex"), sem("parts"), sem("hi"), sem("lo"), sem("stk")
        s_kvo, s_kT = sem("kv_scaled"), sem("keysT_sb")
        s_stored = [sem("stored0"), sem("stored1")]
        block = ctx.enter_context(nc.Block())

        @block.sync
        def _(sp):
            sp.dma_start(ident[:, :], t["ident"]).then_inc(s_c, 16)
            sp.dma_start(wqpk[:, :, :], t["wqpk"].rearrange("d (k n) -> d k n", k=4)).then_inc(s_c, 16)
            sp.dma_start(sel[:, :, :, :], t["sel"].rearrange("r (o s m) -> r o s m", o=2, s=8)).then_inc(s_c, 16)
            sp.wait_ge(s_id, 1)
            for blk in range(4):
                for k in range(4):
                    sp.dma_start(pkeys[32 * k:32 * k + 32, blk, k, :],
                                 t["pkeys"][(4 * blk + k) * 32:(4 * blk + k + 1) * 32, :]).then_inc(s_c, 16)
            sp.dma_start(xT[:, :], d["x4T"][:, 0:C3]).then_inc(s_x, 16)
            for k in range(2):
                sp.sem_inc(s_stored[k], 32)
            sp.wait_ge(s_unit, 4)
            with sp.Fori(0, NC) as c:
                sp.dma_start(xT[:, :], d["x4T"].rearrange("o (c n) -> c o n", n=C3)[c + 1]).then_inc(s_x, 16)
                for h in range(H):
                    wait_alone(sp, s_kT, c * H + (h + 1), s_passed)
                    sp.dma_start(d["KT"][h, :, 0:G * P].rearrange("o (c n) -> c o n", n=C3)[c], kT[:, h % 2, :]).then_inc(s_stored[h % 2], 16)
                    sp.dma_start(d["V"][h, 0:G].rearrange("(c t) p o -> c p t o", t=3)[c], kvo[:, h % 2, :, D:2 * D]
                                 ).then_inc(s_stored[h % 2], 16)
            for k in range(2):
                sp.wait_ge(s_stored[k], 32 + 32 * NC * H // 2)

        @block.tensor
        def _(pe):
            def sums(c, n):
                h, kt = (n // KT) % H, n % KT
                v, q = kt // 8, kt % 8
                pe.matmul(psS[:, n % 4, 0:C3], sel[:, v % 2, q, :], stack[:, h % 2, v, :],
                          start=True, stop=True).then_inc(s_sum, 1)

            def unit(c, j, u):
                kind = u[0]
                pe.wait_ge(s_unit_used, c * UNITS + (UNITS_BEFORE + j) if not (type(c) is int) else UNITS_BEFORE + j)
                if kind == "query":
                    if type(c) is int:
                        pe.wait_ge(s_x, 16)
                    else:
                        pe.wait_ge(s_x, c * 16 + 32)
                    mm = pe.matmul(psM[:, 0:C3], wqpk[:, u[1], :], xT[:, :], start=True, stop=True)
                elif kind == "score":
                    _, ti, blk = u
                    mm = pe.matmul(psM[0:P, 0:4 * NK], qpk[:, blk, ti * P:(ti + 1) * P],
                                   pkeys[:, blk, :, :].rearrange("r k n -> r (k n)"), start=True, stop=True)
                elif kind == "kv":
                    wait_alone(pe, s_kvT, c * H + (u[1] + 1 + 2), s_passed)
                    for ti in range(3):
                        mm = pe.transpose(psM[0:P, ti * 128:(ti + 1) * 128], kvT[:, ti * P:(ti + 1) * P], ident[:, :])
                else:
                    wait_alone(pe, s_kvo, c * H + (u[1] + 1), s_passed)
                    for ti in range(3):
                        mm = pe.transpose(psM[0:D, ti * P:(ti + 1) * P], kvo[:, u[1] % 2, ti, 0:D], ident[0:P, 0:P])
                mm.then_inc(s_unit, 1)

            def turn(c, h, ti):
                one = type(c) is int
                if ti == 0:
                    if one:
                        pe.wait_ge(s_stk, h + 1)
                    else:
                        wait_alone(pe, s_stk, c * H + (h + 1), s_passed)
                if one:
                    if ti:
                        pe.wait_ge(s_T_used, 3 * h + ti)
                else:
                    wait_alone(pe, s_T_used, c * (3 * H) + (3 * h + ti), s_passed)
                for v in range(4):
                    mm = pe.transpose(psT[:, v, 0, :], stk[:, h % 2, ti, v:v + 2, :, :].rearrange("p v w e -> p (v w e)"),
                                      ident16[0:P, 0:P])
                mm.then_inc(s_T, 1)

            pe.wait_ge(s_c, 16 * 19)
            for j, u in enumerate(FIRST_UNITS):
                unit(0, j - UNITS_BEFORE, u)
            pe.wait_ge(s_id, 2)
            for ti in range(3):
                turn(0, 0, ti)
            pe.wait_ge(s_T_used, 3)
            for n in range(LA):
                sums(0, n)
            pe.wait_ge(s_tab, 16 * H)
            with pe.Fori(0, NC) as c:
                j = 0
                for h in range(H):
                    for kt in range(KT):
                        n = h * KT + kt
                        if kt == 0:
                            pe.wait_ge(s_kvT, c * H + (h + 1))
                        pe.wait_ge(s_weight, c * (H * KT) + (n + 1))
                        mm = pe.matmul(psKV[:, h % 2, 0:C3], tab[h][:, kt, :], ww[:, n % 4, :],
                                       start=(kt == 0), stop=(kt == KT - 1))
                        if kt == KT - 1:
                            mm.then_inc(s_acc, 1)
                        if kt == KT - LA:
                            pe.wait_ge(s_T_used, c * (3 * H) + 3 * (h + 2))
                        sums(c, n + LA)
                        for u in units_at(h, kt):
                            unit(c, j, u)
                            j += 1
                        if kt in STACK_AT:
                            turn(c, h + 1, STACK_AT[kt])
                for u in LAST_UNITS:
                    unit(c, j, u)
                    j += 1
                assert j == UNITS

        @block.scalar
        def _(act):
            def unit(c, j, u):
                kind = u[0]
                one = type(c) is int
                if kind == "kv":
                    return
                act.wait_ge(s_unit, UNITS_BEFORE + j + 1 if one else c * UNITS + (UNITS_BEFORE + j + 1))
                if kind == "query":
                    act.copy(qpk[:, u[1], :], psM[:, 0:C3]).then_inc(s_unit_used, 1)
                elif kind == "score":
                    _, ti, blk = u
                    if not one:
                        act.wait_ge(s_parts, c * H + 4 * (1 + blk % 2))
                    h0 = 4 * (blk % 2)
                    act.copy(sc[:, ti, blk // 2, h0:h0 + 4, :].rearrange("p h n -> p (h n)"), psM[0:P, 0:4 * NK]
                             ).then_inc(s_unit_used, 1)
                else:
                    h = u[1]
                    act.wait_ge(s_stored[h % 2], c * (16 * H) + 32 * (h // 2 + 1))
                    act.copy(kT[:, h % 2, :], psM[0:D, 0:C3]).then_inc(s_kT, 1)
                    act.wait_ge(s_kT, c * H + (h + 1))
                    act.sem_inc(s_unit_used, 1)

            def from_turn(c, h, ti):
                act.wait_ge(s_T, 3 * h + ti + 1 if type(c) is int else c * (3 * H) + (3 * h + ti + 1))
                act.copy(stack[:, h % 2, :, ti * P:(ti + 1) * P], psT[:, :, 0, :]).then_inc(s_T_used, 1)

            def at(c, s):
                return s + 1 if type(c) is int else c * H + (s + 1)

            def roots(c, s):
                act.wait_ge(s_bound, at(c, s))
                act.activation(e16[:, :, :], c16[:, :, :], ACT.Exp)
                act.activation(thr[:, 2, :], thr[:, 1, :], ACT.Exp).then_inc(s_ex, 1)

            def high(c, s):
                act.wait_ge(s_parts, at(c, s))
                for w in range(2):
                    ins = act.copy(stk[:, s % 2, :, w:w + 3:2, 0, :], ab[:, w, :, :].rearrange("p t (u e) -> p t u e", u=2))
                ins.then_inc(s_hi, 1)

            def low(c, s):
                act.wait_ge(s_lo, at(c, s))
                for w in range(2):
                    act.mul(stk[:, s % 2, :, w:w + 3:2, 1, :], lo32[:, w, :, :].rearrange("p t (u e) -> p t u e", u=2), 2048.0)
                src = ab[:, 0, :, 0:32]
                act.copy(stk[:, s % 2, :, 4, 0, :], src)
                act.mul(stk[:, s % 2, :, 4, 1, :], lo32[:, 0, :, 0:32], 2048.0).then_inc(s_stk, 1)

            act.sem_inc(s_kvT, 2)
            for j, u in enumerate(FIRST_UNITS):
                unit(0, j - UNITS_BEFORE, u)
            for s in range(2):
                roots(0, s)
                high(0, s)
                low(0, s)
            for ti in range(3):
                from_turn(0, 0, ti)
            with act.Fori(0, NC) as c:
                j = 0
                for h in range(H):
                    for kt in range(KT):
                        n = h * KT + kt
                        act.wait_ge(s_sum, c * (H * KT) + (n + 1))
                        act.activation(ew[:, n % 4, :], psS[:, n % 4, 0:C3], ACT.Exp).then_inc(s_exp, 1)
                        if h and kt == ACT_BEHIND + 1:
                            act.wait_ge(s_acc, c * H + h)
                            act.copy(kvT[:, :], psKV[:, (h - 1) % 2, 0:C3]).then_inc(s_kvT, 1)
                        for u in units_at(h, kt - ACT_BEHIND):
                            unit(c, j, u)
                            j += 1
                        if kt - ACT_BEHIND in STACK_AT:
                            from_turn(c, h + 1, STACK_AT[kt - ACT_BEHIND])
                        if kt == 23:
                            roots(c, h + 2)
                        if kt == 25:
                            high(c, h + 2)
                        if kt == 30:
                            low(c, h + 2)
                act.wait_ge(s_acc, c * H + H)
                act.copy(kvT[:, :], psKV[:, 1, 0:C3]).then_inc(s_kvT, 1)
                for u in LAST_UNITS:
                    unit(c, j, u)
                    j += 1

        @block.vector
        def _(dve):
            v = nc.vector
            ch = Chain(dve, s_sel_chain)

            def at(c, s):
                return s + 1 if type(c) is int else c * H + (s + 1)

            def piece(c, s, what):
                h = s % H
                one = type(c) is int
                rows = [(ti, w) for ti in range(3) for w in range(2)]
                ch.join()
                if what == "max0" and not one:
                    if s >= H:
                        wait_alone(dve, s_unit_used, c * UNITS + (UNITS_BEFORE + SCORES_A), s_passed)
                    elif s == 4:
                        wait_alone(dve, s_unit_used, c * UNITS + (UNITS_BEFORE + SCORES_B - UNITS), s_passed)
                if what in ("max0", "max1"):
                    for ti, w in rows[3 * int(what[-1]):][:3]:
                        ch.send(v.max(t16[:, ti, w, 0:8], sc[:, ti, w, h, :]))
                elif what in ("drop0", "drop1"):
                    for ti, w in rows[3 * int(what[-1]):][:3]:
                        ch.send(v.match_replace(tmp[:, ti, w, :], t16[:, ti, w, 0:8], sc[:, ti, w, h, :], -3.0e38))
                elif what in ("next0", "next1"):
                    for ti, w in rows[3 * int(what[-1]):][:3]:
                        ch.send(v.max(t16[:, ti, w, 8:16], tmp[:, ti, w, :]))
                elif what == "shift":
                    if not one:
                        wait_alone(dve, s_stk, c * H + s, s_passed)
                    elif s:
                        dve.wait_ge(s_stk, s)
                    for w in range(2):
                        top = t16[:, :, w, 0:1]
                        ch.send(v.tensor_tensor(tr[:, :, w, :], t16[:, :, w, :], top.to_broadcast([P, 3, TOPK]), ALU.subtract))
                        ch.send(v.tensor_tensor(ab[:, w, :, :], sc[:, :, w, h, :], top.to_broadcast([P, 3, NK]), ALU.subtract))
                elif what == "sums":
                    o = 0
                    for a, na, nb in CAND:
                        dst = cand[:, :, o:o + na * nb].rearrange("p t (a b) -> p t a b", a=na)
                        ch.send(v.tensor_tensor(dst, tr[:, :, 0, a:a + na].unsqueeze(3).to_broadcast([P, 3, na, nb]),
                                                tr[:, :, 1, 0:nb].unsqueeze(2).to_broadcast([P, 3, na, nb]), ALU.add))
                        o += na * nb
                elif what == "smax":
                    for ti in range(3):
                        ch.send(v.max(c16[:, ti, 0:8], cand[:, ti, :]))
                elif what == "sdrop":
                    for ti in range(3):
                        ch.send(v.match_replace(ctmp[:, ti, :], c16[:, ti, 0:8], cand[:, ti, :], -3.0e38))
                elif what == "snext":
                    for ti in range(3):
                        ch.send(v.max(c16[:, ti, 8:16], ctmp[:, ti, :]))
                elif what == "bound":
                    ch(v.tensor_scalar(thr[:, 0, :], c16[:, :, TOPK - 1], 1.0 + 2.0 ** -20, -(2.0 ** -16), ALU.mult, ALU.add))
                    ch(v.tensor_scalar(thr[:, 0, :], thr[:, 0, :], -87.0, None, ALU.max))
                    v.tensor_scalar(thr[:, 1, :], thr[:, 0, :], SHIFT, None, ALU.add).then_inc(s_bound, 1)
                    if one:
                        dve.wait_ge(s_bound, at(c, s))
                    else:
                        wait_alone(dve, s_bound, at(c, s), s_passed)
                elif what == "parts":
                    ch(v.tensor_tensor(ab[:, 0, :, :], ab[:, 0, :, :], thr[:, 1, :].unsqueeze(2).to_broadcast([P, 3, NK]), ALU.subtract))
                    if not one:
                        wait_alone(dve, s_T, c * (3 * H) + 3 * (s - 1), s_passed)
                    v.tensor_scalar(ab[:, :, :, :], ab[:, :, :, :], -30000.0, None, ALU.max).then_inc(s_parts, 1)
                elif what == "low":
                    if one:
                        dve.wait_ge(s_hi, at(c, s))
                    else:
                        wait_alone(dve, s_hi, at(c, s), s_passed)
                    for w in range(2):
                        ins = v.tensor_tensor(lo32[:, w, :, :].rearrange("p t (u e) -> p t u e", u=2),
                                              ab[:, w, :, :].rearrange("p t (u e) -> p t u e", u=2),
                                              stk[:, s % 2, :, w:w + 3:2, 0, :], ALU.subtract)
                    ins.then_inc(s_lo, 1)
                elif what == "scale":
                    if one:
                        dve.wait_ge(s_ex, at(c, s))
                    else:
                        wait_alone(dve, s_ex, at(c, s), s_passed)
                    ch(v.tensor_reduce(rz[:, :], e16[:, :, :], AX_X, ALU.add))
                    ch(v.reciprocal(rz[:, :], rz[:, :]))
                    ch.send(v.tensor_tensor(scale[:, s % 4, :], thr[:, 2, :], rz[:, :], ALU.mult))

            def unit(c, j, u):
                if u[0] != "kv":
                    return
                h = u[1]
                ch.join()
                dve.wait_ge(s_stored[h % 2], c * (16 * H) + 32 * (h // 2 + 1))
                dve.wait_ge(s_unit, c * UNITS + (UNITS_BEFORE + j + 1))
                v.tensor_tensor(kvo[:, h % 2, :, :], psM[0:P, 0:3 * 128].rearrange("p (t n) -> p t n", t=3),
                                scale[:, h % 4, :].unsqueeze(2).to_broadcast([P, 3, 128]), ALU.mult).then_inc(s_kvo, 1)
                dve.wait_ge(s_kvo, c * H + (h + 1))
                dve.sem_inc(s_unit_used, 1)

            v.memset(pkeys[:, :, :, :], 0.0).then_inc(s_id, 1)
            dve.wait_ge(s_c, 16 * 19)
            v.tensor_copy(ident16[:, :], ident[:, :]).then_inc(s_id, 1)
            dve.wait_ge(s_unit_used, UNITS_BEFORE)
            for s in range(2):
                for what in PIECES.values():
                    piece(0, s, what)
            ch.restart()
            with dve.Fori(0, NC) as c:
                j = 0
                for h in range(H):
                    for kt in range(KT):
                        n = h * KT + kt
                        dve.wait_ge(s_exp, c * (H * KT) + (n + 1))
                        v.scalar_tensor_tensor(ww[:, n % 4, :], psS[:, n % 4, 0:C3], -SHIFT, ew[:, n % 4, :],
                                               ALU.is_ge, ALU.mult).then_inc(s_weight, 1)
                        for u in units_at(h, kt - DVE_BEHIND):
                            unit(c, j, u)
                            j += 1
                        if kt in PIECES:
                            piece(c, h + 2, PIECES[kt])
                for u in LAST_UNITS:
                    unit(c, j, u)
                    j += 1
                ch.restart()


NU = NI * (NI // 3 + 1) // 2
ROW_UNITS = [(i, kc) for i in range(NI) for kc in range(i // 3 + 1)]
COL_UNITS = [(j, qc) for qc in range(NI // 3) for j in range(3 * qc + 3)]


LAST_OF_GROUP = [2, 8, NU - 1]


def attention_order():
    first = [("query", 0, k) for k in range(3)] + [("row", 0, u) for u in range(NU)]
    first += [("turn", 0, 0), ("turn", 0, 1), ("col", 0, 0), ("col", 0, 1)]
    o = []
    for h in range(H):
        rows = 0
        for u in range(NU):
            o.append(("pv", h, u))
            if u in LAST_OF_GROUP:
                o.append(("copy", h, LAST_OF_GROUP.index(u)))
            if u in (4, 10):
                o.append(("out", h, (4, 10).index(u)))
            if u == 1 and h:
                o.append(("out", h - 1, 2))
            o.append(("col", h + (u + 2) // NU, (u + 2) % NU))
            if u < 3:
                o.append(("query", h + 1, u))
            if u == 4:
                o.append(("turn", h, 2))
            while rows < min(NU, u * 6 // 5):
                o.append(("row", h + 1, rows))
                rows += 1
            if u in (8, 12):
                o.append(("turn", h + 1, (8, 12).index(u)))
    o.append(("out", H - 1, 2))
    return first, o


def misc_at(kind, h, u):
    if kind == "query":
        return u if h == 0 else 6 * h - 1 + u
    return 6 * h + 3 + u if u < 2 else 6 * (h + 1) + 2


def attention(nc, t, d, out):
    with ExitStack() as ctx:
        sb, ps, sem = pool_of(ctx, nc, "attn")
        NB = 4
        ident, ident_b = sb("ident", [128, 128]), sb("ident_b", [128, 128], BF16)
        causal, causal_b = sb("causal", [P, 2, P]), sb("causal_b", [P, 2, P], BF16)
        xb = sb("xb", [D, PAD])
        wq, wo = sb("wq", [D, NB, D]), sb("wo", [D + 1, NB, D + 1])
        kA, qA = sb("kA", [D + 1, NB, PAD]), sb("qA", [D + 1, 2, PAD])
        vA = sb("vA", [P, NB, NI, D + 1])
        mx, m3 = sb("mx", [P, NI, NI // 3]), sb("m3", [P, NI])
        nm = sb("nm", [P, NI, D + 1])
        ex = sb("ex", [P, 3, C3])
        oT = sb("oT", [D + 1, 2, C3])
        rz, yh = sb("rz", [P, 3]), sb("yh", [P, 3, D])
        y, res, final = sb("y", [P, NI, D]), sb("res", [P, NI, D]), sb("final", [P, NI, D])
        psA, psB, psO = ps("psA", [128, 2, 512]), ps("psB", [128, 2, 512]), ps("psO", [128, 2, 512])
        psM, psY = ps("psM", [128, 512]), ps("psY", [128, 512])
        s_c, s_set, s_bf, s_passed = sem("consts_in"), sem("buffers_set"), sem("bf16_set"), sem("waits_passed")
        s_in = [sem(f"head_in{k}") for k in range(NB)]
        s_pad, s_x, s_q, s_done = sem("pad_written"), sem("x_in"), sem("queries_made"), sem("head_done")
        s_misc, s_misc_used = sem("misc"), sem("misc_used")
        s_row, s_row_used, s_neg = sem("row"), sem("row_used"), sem("maxima")
        s_col, s_exp, s_pv = sem("col"), sem("exps"), sem("pv")
        s_o, s_oT, s_y, s_y_used = sem("o"), sem("oT"), sem("y"), sem("y_used")
        s_res, s_final, s_stored, s_chain = sem("residual_in"), sem("final"), sem("stored"), sem("dve_chain")
        block = ctx.enter_context(nc.Block())
        first, order = attention_order()
        N_U, N_3, N_M = H * NU, 3 * H, 6 * H

        @block.sync
        def _(sp):
            sp.dma_start(ident[:, :], t["ident"]).then_inc(s_c, 16)
            sp.dma_start(causal[:, :, :], t["causal"]).then_inc(s_c, 16)
            sp.wait_ge(s_set, 5)
            sp.sem_inc(s_done, NB)
            sp.dma_start(d["KT"][0, :, G * P:], d["KT"][0, :, 0:P]).then_inc(s_pad, 16)
            sp.dma_start(d["V"][0, G:G + 1], d["V"][0, 0:1]).then_inc(s_pad, 16)
            sp.wait_ge(s_pad, 32)

            def load_x(b, ahead):
                src = d["x4T"][:, ahead * P:(ahead + G) * P].rearrange("o (i b p) -> b o i p", b=B, p=P)
                sp.dma_start(xb[:, :].rearrange("o (i p) -> o i p", p=P), src[b]).then_inc(s_x, 16)

            def load_head(b, ahead, h, w):
                kt = d["KT"][h, :, ahead * P:(ahead + G) * P].rearrange("o (i b p) -> b o i p", b=B, p=P)
                sp.dma_start(kA[0:D, w, :].rearrange("o (i p) -> o i p", p=P), kt[b]).then_inc(s_in[w], 16)
                vt = d["V"][h, ahead:ahead + G].rearrange("(i b) p o -> b p i o", b=B)
                sp.dma_start(vA[:, w, :, 0:D], vt[b]).then_inc(s_in[w], 16)
                sp.dma_start(wq[:, w, :], t["wq"][h]).then_inc(s_in[w], 16)
                sp.dma_start(wo[0:D, w, 0:D], t["wo"][h]).then_inc(s_in[w], 16)

            load_x(0, 0)
            load_head(0, 0, 0, 0)
            with sp.Fori(0, B) as b:
                for h in range(1, H + 1):
                    if h == H:
                        wait_alone(sp, s_q, b * H + H, s_passed)
                        load_x(b, 1)
                    wait_alone(sp, s_done, b * H + (h + 1), s_passed)
                    load_head(b, h // H, h % H, h % NB)

        @block.gpsimd
        def _(pool):
            v = nc.gpsimd
            set_one = Chain(pool, s_set)
            set_one(v.memset(kA[D:D + 1, :, :], 1.0))
            set_one(v.memset(vA[:, :, :, :], 1.0))
            set_one(v.memset(nm[:, :, :], 0.0))
            set_one(v.memset(wo[:, :, :], 0.0))
            set_one(v.memset(wo[D:D + 1, :, D:D + 1], 1.0))
            with pool.Fori(0, B) as b:
                pool.dma_start(res[:, :, :], d["h2"].rearrange("i p b o -> b p i o")[b]).then_inc(s_res, 16)
                wait_alone(pool, s_final, b * 3 + 6, s_passed)
                pool.dma_start(out[b, 0:(NI - 1) * P, :].rearrange("(i p) o -> p i o", p=P), final[:, 0:NI - 1, :]).then_inc(s_stored, 16)
                pool.dma_start(out[b, (NI - 1) * P:SEQ, :], final[0:P - 1, NI - 1, :]).then_inc(s_stored, 16)
                wait_alone(pool, s_stored, b * 32 + 32, s_passed)

        @block.tensor
        def _(pe):
            pe.wait_ge(s_c, 32)
            pe.wait_ge(s_set, 5)
            pe.wait_ge(s_bf, 2)
            def steps(b, order):
                for kind, h, u in order:
                    k, w, n = h % 2, h % NB, h * NU + u
                    if kind in ("query", "turn"):
                        wait_alone(pe, s_misc_used, b * N_M + (misc_at(kind, h, u) + 1), s_passed)
                        if kind == "query":
                            if u == 0:
                                wait_alone(pe, s_x, b * 16 + 16 * (1 + h // H), s_passed)
                                wait_alone(pe, s_in[w], b * (64 * H // NB) + 64 * (h // NB + 1), s_passed)
                            mm = pe.matmul(psM[0:D, 0:C3], wq[:, w, :], xb[:, u * C3:(u + 1) * C3], start=True, stop=True)
                        else:
                            pe.wait_ge(s_neg, b * N_3 + (3 * h + u + 1))
                            for ti in range(3):
                                mm = pe.matmul(psM[0:D + 1, ti * P:(ti + 1) * P], nm[:, 3 * u + ti, :], ident[0:P, 0:P],
                                               start=True, stop=True)
                        mm.then_inc(s_misc, 1)
                    elif kind == "row":
                        i, kc = ROW_UNITS[u]
                        if u < 3 or u in (3, 9):
                            pe.wait_ge(s_misc_used, b * N_M + (misc_at("query", h, i // 3) + 2))
                        pe.wait_ge(s_row_used, b * N_U + (n + 1))
                        cols = min(3, i + 1 - 3 * kc) * P
                        diag = kc == i // 3
                        mm = pe.matmul(psA[0:P, n % 2, 0:cols], qA[0:D, k, i * P:(i + 1) * P],
                                       kA[0:D, w, kc * C3:kc * C3 + cols], start=True, stop=not diag)
                        if diag:
                            mm = pe.matmul(psA[0:P, n % 2, cols - P:cols], ident_b[0:P, 0:P], causal_b[:, 0, :],
                                           start=False, stop=True)
                        mm.then_inc(s_row, 1)
                    elif kind == "col":
                        j, qc = COL_UNITS[u]
                        if u in (0, 3, 9):
                            pe.wait_ge(s_misc_used, b * N_M + (misc_at("turn", h, qc) + 2))
                        pe.wait_ge(s_exp, b * N_U + (n + 1))
                        i0 = max(j, 3 * qc)
                        cols = (3 * qc + 3 - i0) * P
                        diag = j >= 3 * qc
                        mm = pe.matmul(psB[0:P, n % 2, 0:cols], kA[:, w, j * P:(j + 1) * P],
                                       qA[:, k, i0 * P:(3 * qc + 3) * P], start=True, stop=not diag)
                        if diag:
                            mm = pe.matmul(psB[0:P, n % 2, 0:P], ident_b[0:P, 0:P], causal_b[:, 1, :], start=False, stop=True)
                        mm.then_inc(s_col, 1)
                    elif kind == "pv":
                        j, qc = COL_UNITS[u]
                        m = 3 * h + qc
                        if j == 0:
                            pe.wait_ge(s_oT, b * N_3 + (m + 1))
                        pe.wait_ge(s_exp, b * N_U + (n + 3))
                        i0 = max(j, 3 * qc)
                        cols = (3 * qc + 3 - i0) * P
                        pe.matmul(psO[0:D + 1, m % 2, C3 - cols:C3], vA[:, w, j, :], ex[:, n % 3, 0:cols],
                                  start=(j == 0), stop=(j == 3 * qc + 2)).then_inc(s_pv, 1)
                    elif kind == "out":
                        m = 3 * h + u
                        pe.wait_ge(s_y_used, b * N_3 + (m + 1))
                        pe.wait_ge(s_oT, b * N_3 + (m + 3))
                        for ti in range(3):
                            mm = pe.matmul(psY[0:P, ti * (D + 1):(ti + 1) * (D + 1)], oT[:, m % 2, ti * P:(ti + 1) * P],
                                           wo[:, w, :], start=True, stop=True)
                        mm.then_inc(s_y, 1)

            steps(0, first)
            with pe.Fori(0, B) as b:
                steps(b, order)

        @block.scalar
        def _(act):
            act.sem_inc(s_exp, 2)
            act.sem_inc(s_misc_used, 1)
            act.sem_inc(s_oT, 2)
            def steps(b, order):
                for kind, h, u in order:
                    k, n = h % 2, h * NU + u
                    if kind == "query":
                        act.wait_ge(s_misc, b * N_M + (misc_at(kind, h, u) + 1))
                        act.mul(qA[0:D, k, u * C3:(u + 1) * C3], psM[0:D, 0:C3], D ** -0.5).then_inc(s_misc_used, 1)
                        if u == 2:
                            act.sem_inc(s_q, 1)
                    elif kind == "turn":
                        act.wait_ge(s_misc, b * N_M + (misc_at(kind, h, u) + 1))
                        act.copy(qA[D:D + 1, k, u * C3:(u + 1) * C3], psM[D:D + 1, 0:C3]).then_inc(s_misc_used, 1)
                    elif kind == "col":
                        j, qc = COL_UNITS[u]
                        cols = (3 * qc + 3 - max(j, 3 * qc)) * P
                        act.wait_ge(s_col, b * N_U + (n + 1))
                        act.wait_ge(s_pv, b * N_U + (n + 1))
                        act.activation(ex[:, n % 3, 0:cols], psB[0:P, n % 2, 0:cols], ACT.Exp).then_inc(s_exp, 1)
                    elif kind == "copy":
                        m = 3 * h + u
                        act.wait_ge(s_pv, b * N_U + (h * NU + LAST_OF_GROUP[u] + 4))
                        act.wait_ge(s_y, b * N_3 + (m + 1))
                        act.copy(oT[:, m % 2, :], psO[0:D + 1, m % 2, 0:C3]).then_inc(s_oT, 1)

            steps(0, first)
            with act.Fori(0, B) as b:
                steps(b, order)

        @block.vector
        def _(dve):
            c = Chain(dve, s_chain)
            v = nc.vector
            dve.wait_ge(s_c, 32)
            v.tensor_copy(ident_b[:, :], ident[:, :]).then_inc(s_bf, 1)
            v.tensor_copy(causal_b[:, :, :], causal[:, :, :]).then_inc(s_bf, 1)
            dve.sem_inc(s_row_used, 2)
            dve.sem_inc(s_y_used, 1)
            dve.sem_inc(s_pv, 3)
            dve.sem_inc(s_y, 2)
            dve.sem_inc(s_final, 3)
            def steps(b, order):
                for kind, h, u in order:
                    k, n = h % 2, h * NU + u
                    if kind == "row":
                        i, kc = ROW_UNITS[u]
                        cols = min(3, i + 1 - 3 * kc) * P
                        dve.wait_ge(s_row, b * N_U + (n + 1))
                        v.tensor_reduce(mx[:, i, kc:kc + 1], psA[0:P, n % 2, 0:cols], AX_X, ALU.max).then_inc(s_row_used, 1)
                        if i % 3 == 2 and kc == i // 3:
                            r = i // 3
                            tiles = slice(3 * r, 3 * r + 3)
                            dve.wait_ge(s_row_used, b * N_U + (n + 3))
                            c(v.tensor_reduce(m3[:, tiles], mx[:, tiles, 0:r + 1], AX_X, ALU.max))
                            if h:
                                dve.wait_ge(s_misc, b * N_M + (misc_at("turn", h - 1, r) + 1))
                            v.tensor_scalar(nm[:, tiles, D], m3[:, tiles], -1.0, None, ALU.mult).then_inc(s_neg, 1)
                    elif kind == "out":
                        m = 3 * h + u
                        tiles = slice(3 * u, 3 * u + 3)
                        dve.wait_ge(s_y, b * N_3 + (m + 3))
                        yv = psY[0:P, 0:3 * (D + 1)].rearrange("p (t e) -> p t e", t=3)
                        c(v.reciprocal(rz[:, :], yv[:, :, D]))
                        if h == 0:
                            dve.wait_ge(s_final, b * 3 + (u + 1))
                        v.tensor_tensor((yh[:, :, :] if h else y[:, tiles, :]), yv[:, :, 0:D],
                                        rz[:, :].unsqueeze(2).to_broadcast([P, 3, D]), ALU.mult).then_inc(s_y_used, 1)
                        dve.wait_ge(s_y_used, b * N_3 + (m + 2))
                        if h:
                            c(v.tensor_tensor(y[:, tiles, :], y[:, tiles, :], yh[:, :, :], ALU.add))
                        if h == H - 1:
                            dve.wait_ge(s_res, b * 16 + 16)
                            v.tensor_tensor(final[:, tiles, :], y[:, tiles, :], res[:, tiles, :], ALU.add).then_inc(s_final, 1)
                        if u == 2:
                            dve.sem_inc(s_done, 1)

            steps(0, first)
            c.restart()
            with dve.Fori(0, B) as b:
                steps(b, order)
                c.restart()


def count_units():
    n, last = 0, {}
    for h in range(H):
        for kt in range(KT):
            for u in units_at(h, kt):
                n += 1
                if u[0] == "score":
                    last[u[2] % 2] = n
    return last[0], last[1]


SCORES_A, SCORES_B = count_units()


def lay_out(a):
    def c(x):
        return np.ascontiguousarray(x)

    o = {}
    o["x"] = lay_out_x(a["x"])
    o["cls_tok"] = c(a["cls_tok"][0])
    o["L0_tok_W"] = c(a["L0_tok_W"].reshape(D, 2, PATCH // 2 + 1, C_IN).transpose(1, 2, 3, 0).reshape(18, C_IN * D))
    eo = np.concatenate([np.arange(0, D, 2), np.arange(1, D, 2)])
    o["wqk"] = c(np.concatenate([a["L0_attn_W_Q"][:, eo], a["L0_attn_W_K"][:, eo]], 1))
    o["wv"] = c(a["L0_attn_W_V"])
    o["gate_w"], o["gate_b"] = c(a["L0_ffn_gate_w"]), c(a["L0_ffn_gate_b"][None])
    o["w1"], o["b1"] = c(a["L0_ffn_w1"].transpose(1, 0, 2)), c(a["L0_ffn_b1"].T)
    o["w2"], o["b2"] = c(a["L0_ffn_w2"].transpose(1, 0, 2)), c(a["L0_ffn_b2"])
    o["ln_g"], o["ln_b"] = c(a["L0_ffn_gamma"][None]), c(a["L0_ffn_beta"][None])
    w = a["L1_attn_W_qkv"].reshape(16, 3, 4, D)
    bq = a["L1_attn_b_qkv"].reshape(16, 3, 4)
    o["wq3"] = c(w[:, 0].reshape(D, D).T)
    o["wkv3"] = c(w[:, 1:].transpose(1, 0, 2, 3).reshape(2 * D, D).T)
    o["bq3"] = c(bq[:, 0].reshape(D, 1))
    o["bkv3"] = c(bq[:, 1:].transpose(1, 0, 2).reshape(1, 2 * D))
    for k, n in (("hln_w", "w"), ("hln_b", "b")):
        o[k] = c(np.concatenate([a["L1_attn_kln_" + n].reshape(1, D), a["L1_attn_vln_" + n].reshape(1, D)], 1))
    o["wp3"], o["bp3"] = c(a["L1_attn_W_proj"].T), c(a["L1_attn_b_proj"][None])
    o["wqpk"] = c(a["L1_ffn_Wq_pk"])
    keys = a["L1_ffn_pk_keys"].transpose(0, 2, 3, 1)
    o["pkeys"] = c(keys.reshape(2 * H * 32, NK))
    o["wq"] = c(a["L1_ffn_Wq"].reshape(D, H, D).transpose(1, 0, 2))
    o["wo"] = c(a["L1_ffn_Wo"].reshape(H, D, D))
    tab = np.concatenate([a["L1_ffn_keys_table"], a["L1_ffn_values_table"]], 1)
    tab = tab.reshape(H, 2, 8, 4, 2, 32, 2 * D)
    tab = np.stack([tab[:, 0, :, :, 0], tab[:, 0, :, :, 1], tab[:, 1, :, :, 1], tab[:, 1, :, :, 0]], 1)
    o["table"] = c(tab.transpose(3, 4, 0, 1, 2, 5).reshape(128, H, KT, 2 * D))
    return o


def build(nc, t, out):
    d = {}
    for name, shape in (("gw", [PATCH, C_IN * D]), ("h0", [B, PAD, D]), ("h1", [NI, P, B, D]), ("x3", [NI, P, B, D]),
                        ("x3T", [NI, D, 2, HALF]), ("q3T", [NI, D, 2, HALF]), ("h2", [NI, P, B, D]),
                        ("x4T", [D, (NC + 1) * C3]), ("KT", [H, D, (G + 1) * P]), ("V", [H, G + 1, P, D])):
        d[name] = nc.dram_tensor("scratch_" + name, shape, F32, kind="Internal").ap()
    with ExitStack() as ctx:
        kvs = ctx.enter_context(nc.sbuf_tensor("kv_sums", [D, B, D], F32))
        tab = [ctx.enter_context(nc.sbuf_tensor(f"table{h}", [128, KT, 2 * D], F32)) for h in range(H)]
        s_tab = ctx.enter_context(nc.semaphore("table_in"))
        with nc.Block() as block:
            @block.gpsimd
            def _(pool):
                for h in range(H):
                    pool.dma_start(tab[h][:, :, :], t["table"][:, h, :, :]).then_inc(s_tab, 16)
        embed(nc, t, d)
        layer0_and_kv(nc, t, d, kvs)
        linear_attention(nc, t, d, kvs)
        memory(nc, t, d, tab, s_tab)
    attention(nc, t, d, out)


def kernel(**inputs):
    from concourse import bacc, bass_utils

    arrays = {**lay_out({k: np.asarray(v) for k, v in inputs.items()}), **constants()}
    nc = bacc.Bacc("TRN2", target_bir_lowering=False, num_devices=1)
    t = {k: nc.dram_tensor(f"in_{k}_dram", a.shape, mybir.dt.from_np(a.dtype), kind="ExternalInput").ap()
         for k, a in arrays.items()}
    out = nc.dram_tensor("out_dram", (B, SEQ, D), F32, kind="ExternalOutput").ap()
    build(nc, t, out)
    result = bass_utils.run_bass_kernel_spmd(nc, [{f"in_{k}_dram": a for k, a in arrays.items()}], core_ids=[0])
    return result.results[0]["out_dram"]
```

```python
from contextlib import ExitStack

import numpy as np

import concourse.bass as bass
import concourse.mybir as mybir
from concourse.alu_op_type import AluOpType as ALU

F32 = mybir.dt.float32
F16 = mybir.dt.float16
BF16 = mybir.dt.bfloat16
ACT = mybir.ActivationFunctionType
AX_X = mybir.AxisListType.X

B, C_IN, T_IN, V_IN = 8, 64, 128, 64
D = 64
PATCH, STRIDE = 16, 8
NPATCH = T_IN // STRIDE
SEQ = 1 + V_IN * NPATCH
P = 114
NI = 9
PAD = NI * P
G = NI * B
HALF = 4 * P
EPS = 1e-5
NE, F = 16, 128
GAMMA = 0.96875
H = 8
NK = 64
TOPK = 16
C3 = 3 * P
NC = G // 3
SHIFT = 40.0
NEG = -1.0e30

CAND = [(0, 1, 16), (1, 1, 8), (2, 2, 5), (4, 4, 3), (8, 8, 1)]
NCAND = sum(n * m for _, n, m in CAND)


def constants():
    c = {}
    c["ident"] = np.eye(128, dtype=np.float32)
    k = np.arange(PATCH)[None, :] * np.arange(PATCH // 2 + 1)[:, None] * (2 * np.pi / PATCH)
    c["dft"] = (np.concatenate([np.cos(k), -np.sin(k)]) / np.sqrt(PATCH)).astype(np.float32)
    inv = (np.float32(1.0) / np.float32(10000.0) ** (np.arange(0, D, 2, dtype=np.float32) / np.float32(D))).astype(np.float32)
    ang = np.arange(PAD + P, dtype=np.float32)[:, None] * inv[None, :]
    cs = np.stack([np.cos(ang), np.sin(ang)], 1).astype(np.float32)
    c["rope"] = np.ascontiguousarray(cs.reshape(NI + 1, P, 2 * 32))
    m, n = np.arange(P)[:, None], np.arange(P)[None, :]
    lg = np.log(GAMMA)
    c["decay"] = np.where(n >= m, np.exp(np.maximum(n - m, 0) * lg), 0.0).astype(np.float32)
    p = np.arange(P)
    c["edge"] = np.stack([np.exp((p + 1) * lg), np.exp((P - 1 - p) * lg)], 1).astype(np.float32)
    valid = np.ones((NI + 1, P, 1), np.float32) / SEQ
    valid[NI - 1, P - 1] = 0.0
    c["valid"] = valid
    hd = np.arange(D) // 4
    c["headmask"] = (hd[:, None] == hd[None, :]).astype(np.float32)
    c["causal"] = np.stack([np.where(n > m, NEG, 0.0), np.where(n < m, NEG, 0.0)], 1).astype(np.float32)
    sel = np.zeros((2, 2, 64, 8, 4, 32), np.float16)
    for s in range(8):
        for jj in range(4):
            for ii in range(32):
                for o in range(2):
                    for part, size in enumerate((1.0, 2.0 ** -11)):
                        sel[o, o, 32 * part + ii, s, jj, ii] = size
                        sel[o, 1 - o, 32 * part + 4 * s + jj, s, jj, ii] = size
    c["sel"] = np.ascontiguousarray(sel.reshape(2, 128, 8 * 128).transpose(1, 0, 2)).reshape(128, 2 * 8 * 128)
    return c


class Chain:

    def __init__(self, eng, sem):
        self.eng, self.sem, self.n = eng, sem, 0

    def __call__(self, ins):
        self.send(ins)
        self.join()

    def send(self, ins):
        ins.then_inc(self.sem, 1)
        self.n += 1

    def join(self):
        if self.n:
            self.eng.wait_ge(self.sem, self.n)

    def restart(self):
        self.join()
        self.eng.sem_clear(self.sem)
        self.n = 0


def wait_alone(eng, sem, value, passed):
    eng.wait_ge(sem, value)
    eng.sem_inc(passed, 1)


def pool_of(ctx, nc, phase):
    def sb(name, shape, dt=F32):
        return ctx.enter_context(nc.sbuf_tensor(phase + "_sb_" + name, shape, dt))

    def ps(name, shape, dt=F32):
        return ctx.enter_context(nc.psum_tensor(phase + "_" + name, shape, dt))

    def sem(name):
        return ctx.enter_context(nc.semaphore(phase + "_" + name))

    return sb, ps, sem


def embed(nc, t, d):
    with ExitStack() as ctx:
        sb, ps, sem = pool_of(ctx, nc, "embed")
        dft, ident = sb("dft_sb", [18, PATCH]), sb("ident", [D, D])
        wsp = sb("wsp", [18, C_IN * D])
        fold = sb("fold", [PATCH, C_IN * D])
        gw = sb("gw_sb", [128, PATCH // 2, D])
        xt = sb("xt", [128, 2, 4, 17, V_IN])
        oT = sb("oT", [D, 2, 512])
        eo = sb("eo", [128, 2, 8, D])
        psF = ps("psF", [128, 4, 512])
        psT, psE = ps("psT", [128, 2, 512]), ps("psE", [128, 2, 512])
        s_w, s_cls, s_fold, s_foldc, s_gw = sem("weights_in"), sem("cls_stored"), sem("fold_ps"), sem("fold_sb"), sem("gw_in")
        s_x = [sem("x_in0"), sem("x_in1")]
        s_o = [sem("out_stored0"), sem("out_stored1")]
        s_big, s_oT = sem("half_product"), sem("half_product_sb")
        s_ps, s_sb, s_passed = sem("tok_ps"), sem("tok_sb"), sem("waits_passed")
        block = ctx.enter_context(nc.Block())
        xv = t["x"].rearrange("(i k) r n -> i k r n", k=2)
        h0 = d["h0"].rearrange("(i k) s o -> i k s o", k=2)

        @block.sync
        def _(sp):
            sp.dma_start(dft[:, :], t["dft"]).then_inc(s_w, 16)
            sp.dma_start(wsp[:, :], t["L0_tok_W"]).then_inc(s_w, 16)
            sp.dma_start(ident[:, :], t["ident"][0:D, 0:D]).then_inc(s_w, 16)
            for b in range(B):
                sp.dma_start(d["h0"][b, 0:1, :], t["cls_tok"]).then_inc(s_cls, 16)
                sp.dma_start(d["h0"][b, SEQ:PAD + P, :], t["cls_tok"].to_broadcast([P + 1, D])).then_inc(s_cls, 16)
            sp.wait_ge(s_foldc, 8)
            sp.dma_start(d["gw"], fold[:, :]).then_inc(s_gw, 16)
            sp.wait_ge(s_gw, 16)
            for two in range(2):
                sp.dma_start(gw[64 * two:64 * two + 64, :, :],
                             d["gw"].rearrange("(q two) (c o) -> two c q o", two=2, c=C_IN)[two]
                             ).then_inc(s_gw, 16)
            with sp.Fori(0, B // 2) as i:
                ready = [sp.snap(i * 4 + 1), sp.snap(i * 4 + 3)]
                for k in range(2):
                    wait_alone(sp, s_big, ready[k], s_passed)
                    sp.dma_start(xt[:, k, :, :, :], xv[i, k]).then_inc(s_x[k], 16)
            sp.wait_ge(s_cls, 16 * 16)

        @block.tensor
        def _(pe):
            pe.wait_ge(s_w, 48)
            for n in range(8):
                if n >= 4:
                    pe.wait_ge(s_foldc, n - 3)
                nc.tensor.matmul(psF[0:PATCH, n % 4, :], dft[:, :], wsp[:, n * 512:(n + 1) * 512],
                                 start=True, stop=True).then_inc(s_fold, 1)
            pe.wait_ge(s_gw, 48)
            pe.sem_inc(s_big, 3)
            pe.sem_inc(s_ps, 2)

            def product(i, k, half):
                n = 2 * k + half
                pe.wait_ge(s_oT, i * 4 + (n + 1))
                for q in range(PATCH // 2):
                    m0 = 8 * half + q // 4
                    mm = nc.tensor.matmul(psT[0:D, half, :], gw[:, q, :], xt[:, k, q % 4, m0:m0 + 8, :].rearrange("p m v -> p (m v)"),
                                          start=(q == 0), stop=(q == PATCH // 2 - 1))
                mm.then_inc(s_big, 1)

            def turn(i, k, half):
                n = 2 * k + half
                wait_alone(pe, s_sb, i * 4 + (n + 1), s_passed)
                wait_alone(pe, s_oT, i * 4 + (n + 3), s_passed)
                for vt in range(4):
                    mm = pe.transpose(psE[:, half, vt * D:(vt + 1) * D], oT[:, half, vt * 128:(vt + 1) * 128], ident[:, :])
                mm.then_inc(s_ps, 1)

            with pe.Fori(0, B // 2) as i:
                for k in range(2):
                    pe.wait_ge(s_x[k], (i + 1) * 16)
                    for half in range(2):
                        product(i, k, half)
                        if k or half:
                            turn(i, (2 * k + half - 1) // 2, 1 - half)
                turn(i, 1, 1)

        @block.vector
        def _(dve):
            for n in range(8):
                dve.wait_ge(s_fold, n + 1)
                nc.vector.tensor_copy(fold[:, n * 512:(n + 1) * 512], psF[0:PATCH, n % 4, :]).then_inc(s_foldc, 1)
            dve.sem_inc(s_sb, 2)
            with dve.Fori(0, B // 2) as i:
                for k in range(2):
                    for half in range(2):
                        dve.wait_ge(s_o[k], (i + 1) * 32)
                        dve.wait_ge(s_ps, i * 4 + (2 * k + half + 3))
                        nc.vector.tensor_copy(eo[:, k, 4 * half:4 * half + 4, :],
                                              psE[:, half, 0:4 * D]).then_inc(s_sb, 1)

        @block.scalar
        def _(act):
            act.sem_inc(s_oT, 2)
            for k in range(2):
                act.sem_inc(s_o[k], 32)
            with act.Fori(0, B // 2) as i:
                for k in range(2):
                    for half in range(2):
                        n = 2 * k + half
                        act.wait_ge(s_ps, i * 4 + (n + 1))
                        act.wait_ge(s_big, i * 4 + (n + 4))
                        act.copy(oT[:, half, :], psT[0:D, half, :]).then_inc(s_oT, 1)
                for k in range(2):
                    act.wait_ge(s_sb, i * 4 + (2 * k + 4))
                    for n2 in range(2):
                        act.dma_start(h0[i, k, 1:SEQ, :].rearrange("(v vt two) o -> two v vt o", vt=8, two=2)[n2],
                                      eo[64 * n2:64 * n2 + 64, k, :, :]).then_inc(s_o[k], 16)
            for k in range(2):
                act.wait_ge(s_o[k], 32 * (B // 2 + 1))


def lay_out_x(x):
    x = np.concatenate([x] + [x[:, :, -1:, :]] * STRIDE, axis=2)
    x = x.reshape(B, C_IN, 17, 4, 2, V_IN).transpose(0, 4, 1, 3, 2, 5)
    return np.ascontiguousarray(x).reshape(B, 2 * C_IN, 4 * 17 * V_IN)


def layer0_and_kv(nc, t, d, kvs, tab, s_tab):
    with ExitStack() as ctx:
        sb, ps, sem = pool_of(ctx, nc, "layer0")
        ident = sb("ident", [128, 128])
        decay = sb("decay", [P, P])
        edge = sb("edge", [P, 2])
        wqk, wv = sb("wqk", [D, 2 * D]), sb("wv", [D, D])
        gate_w, gate_b = sb("gate_w", [D, NE]), sb("gate_b", [P, NE])
        w1, b1 = sb("w1", [D, NE, F]), sb("b1", [F, NE])
        w2, b2 = sb("w2", [F, NE, D]), sb("b2", [3 * NE, D])
        ln_g, ln_b = sb("ln_g", [P, D]), sb("ln_b", [P, D])
        wq3, wkv3 = sb("wq3", [D, D]), sb("wkv3", [D, 2 * D])
        bq3, bkv3 = sb("bq3", [D, 1]), sb("bkv3", [P, 2 * D])
        hln_w, hln_b = sb("hln_w", [P, 2 * D]), sb("hln_b", [P, 2 * D])
        rope, valid = sb("rope", [P, 2, 32]), sb("valid", [P, 1])
        hin = sb("hin", [P, B, D])
        hb = sb("hb", [P, B, D])
        xn = sb("xn", [P, B, D])
        acc = sb("acc", [P, B, D])
        st = sb("st", [P, 3, B])
        xT = sb("xT", [D, 2, HALF])
        xTb = xT[:, :, :].rearrange("d u (b p) -> d (u b) p", p=P)
        vs = sb("vs", [P, B, D])
        shared = sb("shared", [128, 2, 2 * B * 2 * 32])
        ra = shared[0:P, 0, :].rearrange("p (a w e) -> p a w e", a=2 * B, w=2)
        rb = shared[0:P, 1, :].rearrange("p (a w e) -> p a w e", a=2 * B, w=2)
        hid = shared[:, :, :].rearrange("p a n -> p (a n)")[:, 0:4 * HALF].rearrange("p (k u n) -> p k u n", k=2, u=2)
        qk = sb("qk", [P, B, 2, D])
        x0 = vs
        ks = sb("ks", [P, B, D])
        sq = ks
        qkT = sb("qkT", [D, 2, 2, HALF])
        aT = sb("aT", [P, 2, HALF])
        state = sb("state", [D, B, D])
        lg, ex = sb("lg", [P, B, NE]), sb("ex", [P, B, NE])
        rep, gates = sb("rep", [P, B, NE]), sb("gates", [P, B, NE])
        m8, mt = sb("m8", [P, B, 8]), sb("mt", [P, B, 8])
        gz = sb("gz", [P, B])
        part = sb("part", [P, B, 2, NE], BF16)
        g3 = sb("g3", [P, B, 3 * NE])
        gT, gT_b = sb("gT", [3 * NE, 2, HALF]), sb("gT_b", [3 * NE, 2, HALF], BF16)
        pick = sb("pick", [3 * NE, NE, F], BF16)
        q3T = sb("q3T", [D, 2, HALF])
        kv = shared[0:P, 0, :].rearrange("p (b n) -> p b n", b=B)
        kq = shared[0:P, 1, :].rearrange("p (b n) -> p b n", b=B)
        gs = sb("gs", [P, 2, B * 2 * D // 4])
        psX, psY, psQ = ps("psX", [128, 2, 512]), ps("psY", [128, 2, 512]), ps("psQ", [128, 2, 512])
        psG = ps("psG", [128, 2, 512])
        psV = psG[:, 0, :]

        s_first, s_c, s_passed = sem("first_consts_in"), sem("consts_in"), sem("waits_passed")
        s_load, s_valid = sem("tile_in"), sem("valid_in")
        s_stored, s_storedT = sem("stored"), sem("transposes_stored")
        s_dve = sem("dve_chain")
        s_pe = sem("pe_products")
        s_xn, s_x2, s_x3 = sem("xn"), sem("x2"), sem("x3")
        s_xT, s_x2T, s_x3T = sem("xT"), sem("x2T"), sem("x3T")
        s_qk, s_v, s_qkT, s_aT = sem("qk"), sem("v"), sem("qkT"), sem("aT")
        s_lgm, s_ex, s_gates, s_gT, s_pick = sem("lgm"), sem("ex"), sem("gates"), sem("gT"), sem("pick")
        s_hid, s_h1, s_eo, s_gated = sem("hid"), sem("hid_ps"), sem("expert_added"), sem("hid_gated")
        s_spread, s_mT = sem("gates_spread"), sem("experts_sum")
        s_q3, s_kv, s_kvn, s_pe3 = sem("q3"), sem("kv_summed"), sem("kv_normed"), sem("pe_kv")
        s_free = sem("tile_done")
        s_var, s_std = sem("var"), sem("std")
        moeT = qkT[:, 0, :, :]
        block = ctx.enter_context(nc.Block())
        NPE = 11

        @block.gpsimd
        def _(pool):
            pool.wait_ge(s_c, 16 * 18)
            for h in range(H):
                pool.dma_start(tab[h][:, :, :], t["table"][:, h, :, :]).then_inc(s_tab, 16)

        @block.sync
        def _(sp):
            loads = [(decay, t["decay"]), (edge, t["edge"]), (gate_w, t["gate_w"]),
                     (gate_b, t["gate_b"].to_broadcast([P, NE])), (b1, t["b1"]),
                     (b2[0:NE], t["b2"]), (b2[NE:2 * NE], t["b2"]), (b2[2 * NE:], t["b2"]),
                     (ln_g, t["ln_g"].to_broadcast([P, D])), (ln_b, t["ln_b"].to_broadcast([P, D])),
                     (wq3, t["wq3"]), (wkv3, t["wkv3"]), (bq3, t["bq3"]), (bkv3, t["bkv3"].to_broadcast([P, 2 * D])),
                     (hln_w, t["hln_w"].to_broadcast([P, 2 * D])), (hln_b, t["hln_b"].to_broadcast([P, 2 * D]))]
            h_in = d["h0"].rearrange("b (i p) o -> i p b o", p=P)
            sp.dma_start(hin[:, :, :], h_in[0]).then_inc(s_load, 16)
            sp.dma_start(rope[:, :, :], t["rope"][0]).then_inc(s_load, 16)
            for dst, src in ((ident, t["ident"]), (wqk, t["wqk"]), (wv, t["wv"])):
                sp.dma_start(dst[:, :], src).then_inc(s_first, 16)
            for dst, src in loads:
                sp.dma_start(dst[:, :], src).then_inc(s_c, 16)
            sp.dma_start(w1[:, :, :], t["w1"]).then_inc(s_c, 16)
            sp.dma_start(w2[:, :, :], t["w2"]).then_inc(s_c, 16)
            sp.dma_start(valid[:, :], t["valid"][0]).then_inc(s_valid, 16)
            sp.sem_inc(s_stored, 32)
            sp.sem_inc(s_storedT, 32)
            with sp.Fori(0, NI) as i:
                nxt = sp.snap(i + 1)
                wait_alone(sp, s_x2, nxt, s_passed)
                sp.dma_start(hin[:, :, :], h_in[nxt]).then_inc(s_load, 16)
                sp.dma_start(rope[:, :, :], t["rope"][nxt]).then_inc(s_load, 16)
                wait_alone(sp, s_q3, nxt, s_passed)
                sp.dma_start(d["x3T"][i], xT[:, :, :]).then_inc(s_storedT, 16)
                sp.dma_start(d["q3T"][i], q3T[:, :, :]).then_inc(s_storedT, 16)
                sp.dma_start(d["h1"][i], hb[:, :, :]).then_inc(s_stored, 16)
                sp.dma_start(d["x3"][i], xn[:, :, :]).then_inc(s_stored, 16)
                wait_alone(sp, s_kv, nxt, s_passed)
                sp.dma_start(valid[:, :], t["valid"][nxt]).then_inc(s_valid, 16)
            sp.wait_ge(s_stored, 32 * NI + 32)
            sp.wait_ge(s_storedT, 32 * NI + 32)
            sp.wait_ge(s_load, 32 * NI + 32)
            sp.wait_ge(s_valid, 16 * NI + 16)

        @block.tensor
        def _(pe):
            def to_T(src, into, n=B):
                for b in range(n):
                    mm = pe.transpose(into[0:src.shape[2], b // 4, (b % 4) * P:(b % 4 + 1) * P], src[:, b, :], ident[0:P, 0:P])
                return mm

            pe.wait_ge(s_first, 48)
            with pe.Fori(0, NI) as i:
                nxt = i + 1
                wait_alone(pe, s_xn, nxt, s_passed)
                to_T(x0, psX).then_inc(s_pe, 1)
                wait_alone(pe, s_free, nxt, s_passed)
                pe.wait_ge(s_xT, nxt)
                for b in range(B):
                    mm = pe.matmul(psQ[0:P, b // 4, (b % 4) * 128:(b % 4 + 1) * 128], xTb[:, b, :], wqk[:, :], start=True, stop=True)
                mm.then_inc(s_pe, 1)
                for b in range(B):
                    mm = pe.matmul(psV[0:P, b * D:(b + 1) * D], xTb[:, b, :], wv[:, :], start=True, stop=True)
                mm.then_inc(s_pe, 1)
                wait_alone(pe, s_qk, nxt, s_passed)
                to_T(qk[:, :, 0, :], psX)
                to_T(qk[:, :, 1, :], psY).then_inc(s_pe, 1)
                pe.wait_ge(s_qkT, nxt)
                pe.wait_ge(s_v, nxt)
                for b in range(B):
                    c0 = slice((b % 4) * P, (b % 4 + 1) * P)
                    mm = pe.matmul(psX[0:P, b // 4, c0], qkT[:, 1, b // 4, c0], qkT[:, 0, b // 4, c0], start=True, stop=True)
                mm.then_inc(s_pe, 1)
                for b in range(B):
                    qb = qkT[:, 0, b // 4, (b % 4) * P:(b % 4 + 1) * P]
                    pe.matmul(psV[0:P, b * D:(b + 1) * D], qb, state[:, b, :], start=True, stop=True)
                    mm = pe.matmul(psQ[0:D, 0, b * D:(b + 1) * D], ks[:, b, :], vs[:, b, :], start=True, stop=True)
                mm.then_inc(s_pe, 1)
                pe.wait_ge(s_aT, nxt)
                for b in range(B):
                    mm = pe.matmul(psQ[0:P, 1, b * D:(b + 1) * D], aT[:, b // 4, (b % 4) * P:(b % 4 + 1) * P],
                                   vs[:, b, :], start=True, stop=True)
                mm.then_inc(s_pe, 1)
                pe.wait_ge(s_c, 16 * 18)
                pe.wait_ge(s_pick, 1)
                wait_alone(pe, s_x2, nxt, s_passed)
                to_T(xn, psX).then_inc(s_pe, 1)
                pe.wait_ge(s_x2T, nxt)
                for b in range(B):
                    mm = pe.matmul(psV[0:P, b * NE:(b + 1) * NE], xTb[:, b, :], gate_w[:, :], start=True, stop=True)
                mm.then_inc(s_pe, 1)
                wait_alone(pe, s_gates, nxt, s_passed)
                to_T(g3, psY).then_inc(s_pe, 1)
                wait_alone(pe, s_gT, nxt, s_passed)
                for u in range(2):
                    pe.matmul(psQ[0:D, u, 0:HALF], b2[:, :], gT[:, u, :], start=True, stop=False)
                for e in range(NE + 2):
                    if e < NE:
                        bank = (psX, psY)[e % 2]
                        if e >= 2:
                            pe.wait_ge(s_hid, i * NE + (e - 1))
                        for u in range(2):
                            mm = pe.matmul(bank[:, u, 0:HALF], w1[:, e, :], xT[:, u, :], start=True, stop=True)
                        mm.then_inc(s_h1, 1)
                    if e >= 2:
                        k = e - 2
                        pe.wait_ge(s_gated, i * NE + (k + 1))
                        for u in range(2):
                            mm = pe.matmul(psQ[0:D, u, 0:HALF], w2[:, k, :], hid[:, k % 2, u, :],
                                           start=False, stop=(k == NE - 1))
                        mm.then_inc(s_eo, 1)
                    if e < NE:
                        if e >= 1:
                            pe.wait_ge(s_gated, i * NE + e)
                        for u in range(2):
                            mm = pe.matmul(psG[:, u, 0:HALF], pick[:, e, :], gT_b[:, u, :], start=True, stop=True)
                        mm.then_inc(s_spread, 1)
                wait_alone(pe, s_mT, nxt, s_passed)
                for b in range(B):
                    mm = pe.transpose(psV[0:P, b * D:(b + 1) * D], moeT[:, b // 4, (b % 4) * P:(b % 4 + 1) * P], ident[0:D, 0:D])
                mm.then_inc(s_pe, 1)
                wait_alone(pe, s_x3, nxt, s_passed)
                to_T(xn, psX).then_inc(s_pe3, 1)
                pe.wait_ge(s_x3T, nxt)
                for b in range(B):
                    mm = pe.matmul(psQ[0:P, b // 4, (b % 4) * 128:(b % 4 + 1) * 128], xTb[:, b, :], wkv3[:, :], start=True, stop=True)
                mm.then_inc(s_pe3, 1)
                for u in range(2):
                    mm = pe.matmul(psY[0:D, u, 0:HALF], wq3[:, :], xT[:, u, :], start=True, stop=True)
                mm.then_inc(s_pe3, 1)
                pe.wait_ge(s_kvn, nxt)
                for b in range(B):
                    mm = pe.matmul(psV[0:D, b * D:(b + 1) * D], kv[:, b, 0:D], kv[:, b, D:2 * D], start=True, stop=True)
                mm.then_inc(s_pe3, 1)

        @block.scalar
        def _(act):
            act.wait_ge(s_var, 1)
            act.activation(st[:, 2, :], st[:, 1, :], ACT.Sqrt).then_inc(s_std, 1)
            act.wait_ge(s_c, 16 * 18)
            with act.Fori(0, NI) as i:
                nxt = i + 1

                def products(n):
                    act.wait_ge(s_pe, i * NPE + n)

                def copy_T(src, dst, s, rows=D):
                    for u in range(2):
                        ins = act.copy(dst[0:rows, u, :], src[0:rows, u, 0:HALF])
                    ins.then_inc(s, 1)

                def root(n, x=st[:, 1, :], out=st[:, 2, :]):
                    act.wait_ge(s_var, i * 5 + n)
                    act.activation(out, x, ACT.Sqrt).then_inc(s_std, 1)

                act.wait_ge(s_storedT, i * 32 + 32)
                products(1)
                copy_T(psX, xT, s_xT)
                products(3)
                act.copy(vs[:, :, :], psV[0:P, :]).then_inc(s_v, 1)
                products(4)
                for w in range(2):
                    for u in range(2):
                        ins = act.copy(qkT[:, w, u, :], (psX, psY)[w][0:D, u, 0:HALF])
                ins.then_inc(s_qkT, 1)
                root(2)
                products(8)
                copy_T(psX, xT, s_x2T)
                act.wait_ge(s_lgm, nxt)
                act.activation(ex[:, :, :], lg[:, :, :], ACT.Exp).then_inc(s_ex, 1)
                products(10)
                for u in range(2):
                    act.copy(gT[:, u, :], psY[0:3 * NE, u, 0:HALF])
                    ins = act.copy(gT_b[:, u, :], psY[0:3 * NE, u, 0:HALF])
                ins.then_inc(s_gT, 1)
                for e in range(NE):
                    act.wait_ge(s_h1, i * NE + (e + 1))
                    if e >= 2:
                        act.wait_ge(s_eo, i * NE + (e - 1))
                    for u in range(2):
                        ins = act.activation(hid[:, e % 2, u, :], (psX, psY)[e % 2][:, u, 0:HALF], ACT.Relu, bias=b1[:, e:e + 1])
                    ins.then_inc(s_hid, 1)
                    if e == 9:
                        root(3)
                act.wait_ge(s_eo, i * NE + NE)
                for u in range(2):
                    ins = act.copy(moeT[:, u, :], psQ[0:D, u, 0:HALF])
                ins.then_inc(s_mT, 1)
                root(4)
                root(5)
                act.wait_ge(s_pe3, i * 4 + 1)
                copy_T(psX, xT, s_x3T)
                act.wait_ge(s_pe3, i * 4 + 3)
                for u in range(2):
                    ins = act.activation(q3T[:, u, :], psY[0:D, u, 0:HALF], ACT.Identity, bias=bq3[:, 0:1])
                ins.then_inc(s_q3, 1)
                root(6, gs[:, 0, :], gs[:, 1, :])

        @block.vector
        def _(dve):
            c = Chain(dve, s_dve)
            v = nc.vector
            c.send(v.memset(state[:, :, :], 0.0))
            c.send(v.memset(kvs[:, :, :], 0.0))
            c.send(v.memset(mt[:, :, :], 3.0e38))
            dve.wait_ge(s_first, 48)
            ones = [ident[0:3 * NE, k * NE:(k + 1) * NE].unsqueeze(2).to_broadcast([3 * NE, NE, F]) for k in range(3)]
            c(v.tensor_tensor(pick[:, :, :], ones[0], ones[1], ALU.add))
            c.restart()
            v.tensor_tensor(pick[:, :, :], pick[:, :, :], ones[2], ALU.add).then_inc(s_pick, 1)

            def mean_of(x, out):
                c(v.tensor_reduce(st[:, 0, :], x, AX_X, ALU.add))
                c(v.tensor_scalar(st[:, 0, :], st[:, 0, :], 1.0 / D, None, ALU.mult))

            def centre(x, out):
                c(v.tensor_tensor(out, x, st[:, 0, :].unsqueeze(2).to_broadcast([P, B, D]), ALU.subtract))

            def variance(x, out):
                c(v.tensor_tensor(sq[:, :, :], out, out, ALU.mult))
                c(v.tensor_reduce(st[:, 1, :], sq[:, :, :], AX_X, ALU.add))
                v.tensor_scalar(st[:, 1, :], st[:, 1, :], 1.0 / D, EPS, ALU.mult, ALU.add).then_inc(s_var, 1)

            def scaled(out):
                c(v.reciprocal(st[:, 2, :], st[:, 2, :]))
                return v.tensor_tensor(out, out, st[:, 2, :].unsqueeze(2).to_broadcast([P, B, D]), ALU.mult)

            dve.sem_inc(s_free, 1)
            dve.wait_ge(s_load, 32)
            for part_of_norm in (mean_of, centre, variance):
                part_of_norm(hin[:, :, :], x0[:, :, :])
            dve.wait_ge(s_std, 1)
            scaled(x0[:, :, :]).then_inc(s_xn, 1)
            dve.wait_ge(s_xn, 1)
            c.restart()
            dve.wait_ge(s_c, 16 * 18)
            with dve.Fori(0, NI) as i:
                nxt = i + 1

                def products(n):
                    dve.wait_ge(s_pe, i * NPE + n)

                def norm(x, out, n, done=None):
                    for part_of_norm in (mean_of, centre, variance):
                        part_of_norm(x, out)
                    dve.wait_ge(s_std, i * 5 + n)
                    if done is None:
                        c(scaled(out))
                    else:
                        scaled(out).then_inc(done, 1)
                        dve.wait_ge(done, nxt)

                products(2)
                for u in range(2):
                    src = psQ[0:P, u, :].rearrange("p (a e) -> p a e", e=32)
                    c.send(v.tensor_tensor(ra[:, 8 * u:8 * u + 8, :, :].rearrange("p a w e -> p (a w) e"), src,
                                           rope[:, 0, :].unsqueeze(1).to_broadcast([P, 16, 32]), ALU.mult))
                    c.send(v.tensor_tensor(rb[:, 8 * u:8 * u + 8, :, :].rearrange("p a w e -> p (a w) e"), src,
                                           rope[:, 1, :].unsqueeze(1).to_broadcast([P, 16, 32]), ALU.mult))
                c.join()
                qk4 = qk[:, :, :, :].rearrange("p b w (x e) -> p (b w) x e", x=2)
                c.send(v.tensor_tensor(qk4[:, :, 0, :], ra[:, :, 0, :], rb[:, :, 1, :], ALU.subtract))
                c(v.tensor_tensor(qk4[:, :, 1, :], ra[:, :, 1, :], rb[:, :, 0, :], ALU.add))
                v.tensor_scalar(ks[:, :, :], qk[:, :, 1, :], edge[:, 1:2], None, ALU.mult).then_inc(s_qk, 1)
                products(5)
                for u in range(2):
                    ins = v.tensor_tensor(aT[:, u, :].rearrange("p (b n) -> p b n", b=4),
                                          psX[0:P, u, 0:HALF].rearrange("p (b n) -> p b n", b=4),
                                          decay[:, :].unsqueeze(1).to_broadcast([P, 4, P]), ALU.mult)
                ins.then_inc(s_aT, 1)
                flat = "p b o -> p (b o)"
                products(6)
                dve.wait_ge(s_stored, i * 32 + 32)
                c.send(v.scalar_tensor_tensor(hb[:, :, :].rearrange(flat), psV[0:P, :], edge[:, 0:1],
                                              hin[:, :, :].rearrange(flat), ALU.mult, ALU.add))
                c(v.scalar_tensor_tensor(state[:, :, :].rearrange(flat), state[:, :, :].rearrange(flat), float(GAMMA ** P),
                                         psQ[0:D, 0, :], ALU.mult, ALU.add))
                products(7)
                c(v.tensor_tensor(hb[:, :, :].rearrange(flat), hb[:, :, :].rearrange(flat), psQ[0:P, 1, :], ALU.add))
                norm(hb[:, :, :], xn[:, :, :], 2, s_x2)
                products(9)
                full = [P, B, NE]
                c(v.tensor_tensor(lg[:, :, :], psV[0:P, 0:B * NE].rearrange("p (b e) -> p b e", e=NE),
                                  gate_b[:, :].unsqueeze(1).to_broadcast(full), ALU.add))
                for b in range(B):
                    c.send(v.max(m8[:, b, :], lg[:, b, :]))
                c.join()
                c(v.tensor_copy(mt[:, :, 0:2], m8[:, :, 0:2]))
                for b in range(B):
                    c.send(v.match_replace(rep[:, b, :], mt[:, b, :], lg[:, b, :], -3.0e38))
                c.join()
                c(v.tensor_tensor(rep[:, :, :], rep[:, :, :], lg[:, :, :], ALU.not_equal))
                v.tensor_tensor(lg[:, :, :], lg[:, :, :], m8[:, :, 0:1].to_broadcast(full), ALU.subtract).then_inc(s_lgm, 1)
                dve.wait_ge(s_ex, nxt)
                c(v.tensor_tensor(gates[:, :, :], ex[:, :, :], rep[:, :, :], ALU.mult))
                c(v.tensor_reduce(gz[:, :], gates[:, :, :], AX_X, ALU.add))
                c(v.reciprocal(gz[:, :], gz[:, :]))
                c(v.tensor_tensor(gates[:, :, :], gates[:, :, :], gz[:, :].unsqueeze(2).to_broadcast(full), ALU.mult))
                c(v.tensor_copy(part[:, :, 0, :], gates[:, :, :]))
                c.send(v.tensor_copy(g3[:, :, 0:NE], part[:, :, 0, :]))
                c(v.tensor_tensor(rep[:, :, :], gates[:, :, :], part[:, :, 0, :], ALU.subtract))
                c(v.tensor_copy(part[:, :, 1, :], rep[:, :, :]))
                c(v.tensor_copy(g3[:, :, NE:2 * NE], part[:, :, 1, :]))
                v.tensor_tensor(g3[:, :, 2 * NE:], rep[:, :, :], part[:, :, 1, :], ALU.subtract).then_inc(s_gates, 1)
                for e in range(NE):
                    dve.wait_ge(s_hid, i * NE + (e + 1))
                    dve.wait_ge(s_spread, i * NE + (e + 1))
                    for u in range(2):
                        ins = v.tensor_tensor(hid[:, e % 2, u, :], hid[:, e % 2, u, :], psG[:, u, 0:HALF], ALU.mult)
                    ins.then_inc(s_gated, 1)
                    if e == 6:
                        dve.wait_ge(s_load, i * 32 + 64)
                        mean_of(hin[:, :, :], x0[:, :, :])
                    if e in (7, 8):
                        (centre, variance)[e - 7](hin[:, :, :], x0[:, :, :])
                    if e == 10:
                        dve.wait_ge(s_std, i * 5 + 3)
                        scaled(x0[:, :, :]).then_inc(s_xn, 1)
                        dve.wait_ge(s_xn, nxt + 1)
                products(11)
                c(v.tensor_tensor(acc[:, :, :].rearrange(flat), xn[:, :, :].rearrange(flat), psV[0:P, :], ALU.add))
                norm(acc[:, :, :], acc[:, :, :], 4)
                c(v.tensor_tensor(acc[:, :, :], acc[:, :, :], ln_g[:, :].unsqueeze(1).to_broadcast([P, B, D]), ALU.mult))
                c(v.tensor_tensor(acc[:, :, :], acc[:, :, :], ln_b[:, :].unsqueeze(1).to_broadcast([P, B, D]), ALU.add))
                c(v.tensor_tensor(hb[:, :, :], hb[:, :, :], acc[:, :, :], ALU.add))
                norm(hb[:, :, :], xn[:, :, :], 5, s_x3)
                dve.wait_ge(s_pe3, i * 4 + 2)
                kvg = kv[:, :, :].rearrange("p b (g e) -> p (b g) e", e=4)
                kqg = kq[:, :, :].rearrange("p b (g e) -> p (b g) e", e=4)
                NG = B * 2 * D // 4
                c(v.tensor_tensor(kv[:, :, :], psQ[0:P, :, :].rearrange("p u (b n) -> p (u b) n", b=4),
                                  bkv3[:, :].unsqueeze(1).to_broadcast([P, B, 2 * D]), ALU.add))
                c(v.tensor_reduce(gs[:, 0, :], kvg, AX_X, ALU.add))
                c(v.tensor_scalar(gs[:, 0, :], gs[:, 0, :], 0.25, None, ALU.mult))
                c(v.tensor_tensor(kvg, kvg, gs[:, 0, :].unsqueeze(2).to_broadcast([P, NG, 4]), ALU.subtract))
                c(v.tensor_tensor(kqg, kvg, kvg, ALU.mult))
                c(v.tensor_reduce(gs[:, 0, :], kqg, AX_X, ALU.add))
                v.tensor_scalar(gs[:, 0, :], gs[:, 0, :], 1.0 / 3.0, None, ALU.mult).then_inc(s_var, 1)
                dve.wait_ge(s_std, i * 5 + 6)
                c(v.tensor_scalar(gs[:, 1, :], gs[:, 1, :], EPS, None, ALU.add))
                c(v.reciprocal(gs[:, 1, :], gs[:, 1, :]))
                c(v.tensor_tensor(kvg, kvg, gs[:, 1, :].unsqueeze(2).to_broadcast([P, NG, 4]), ALU.mult))
                c(v.tensor_tensor(kv[:, :, :], kv[:, :, :], hln_w[:, :].unsqueeze(1).to_broadcast([P, B, 2 * D]), ALU.mult))
                c(v.tensor_tensor(kv[:, :, :], kv[:, :, :], hln_b[:, :].unsqueeze(1).to_broadcast([P, B, 2 * D]), ALU.add))
                dve.wait_ge(s_valid, i * 16 + 16)
                v.tensor_scalar(kv[:, :, 0:D], kv[:, :, 0:D], valid[:, 0:1], None, ALU.mult).then_inc(s_kvn, 1)
                dve.wait_ge(s_pe3, i * 4 + 4)
                v.tensor_tensor(kvs[:, :, :].rearrange(flat), kvs[:, :, :].rearrange(flat), psV[0:D, :], ALU.add).then_inc(s_kv, 1)
                wait_alone(dve, s_kv, nxt, s_passed)
                dve.sem_inc(s_free, 1)
                c.restart()


def linear_attention(nc, t, d, kvs):
    with ExitStack() as ctx:
        sb, ps, sem = pool_of(ctx, nc, "linear")
        ident, headmask = sb("ident", [128, 128]), sb("headmask", [D, D])
        wp, bp = sb("wp", [D, D]), sb("bp", [P, D])
        K3 = 3
        hbs, x3s = sb("hb", [P, K3, B, D]), sb("x3", [P, K3, B, D])
        x3Ts, q3Ts = sb("x3T", [D, K3, 2, HALF]), sb("q3T", [D, K3, 2, HALF])
        pbs, ges, xns = sb("pb", [P, K3, B, D]), sb("ge", [P, K3, B, D]), sb("xn", [P, K3, B, D])
        sq, st = sb("sq", [P, K3, B, D]), sb("st", [P, 3, K3, B])
        xTs = sb("xT", [D, K3, 2, HALF])
        psX, psV = ps("psX", [128, K3, 2, 512]), ps("psV", [128, 2, 512])
        s_c, s_passed = sem("consts_in"), sem("waits_passed")
        s_load = [sem(f"tile_in{k}") for k in range(K3)]
        s_store = [sem(f"tile_stored{k}") for k in range(K3)]
        s_dve, s_kvm, s_out, s_ret = sem("dve_chain"), sem("kv_masked"), sem("out_ps"), sem("ret")
        s_proj, s_pb, s_ge, s_var, s_std = sem("proj_ps"), sem("proj_sb"), sem("gelu"), sem("var"), sem("std")
        s_xn, s_xTp, s_xT = sem("xn"), sem("xT_ps"), sem("xT")
        block = ctx.enter_context(nc.Block())

        @block.sync
        def _(sp):
            for dst, src in ((ident, t["ident"]), (headmask, t["headmask"]), (wp, t["wp3"]),
                             (bp, t["bp3"].to_broadcast([P, D]))):
                sp.dma_start(dst[:, :], src).then_inc(s_c, 16)
            for k in range(K3):
                sp.sem_inc(s_store[k], 32)
            with sp.Fori(0, NI // K3) as g:
                for k in range(K3):
                    i = sp.snap(g * K3 + k)
                    wait_alone(sp, s_store[k], g * 32 + 32, s_passed)
                    sp.dma_start(hbs[:, k], d["h1"][i]).then_inc(s_load[k], 16)
                    sp.dma_start(x3s[:, k], d["x3"][i]).then_inc(s_load[k], 16)
                    sp.dma_start(x3Ts[:, k], d["x3T"][i]).then_inc(s_load[k], 16)
                    sp.dma_start(q3Ts[:, k], d["q3T"][i]).then_inc(s_load[k], 16)

        @block.tensor
        def _(pe):
            pe.wait_ge(s_c, 64)
            pe.wait_ge(s_kvm, 1)
            with pe.Fori(0, NI // K3) as g:
                for k in range(K3):
                    nxt = g * K3 + (k + 1)
                    wait_alone(pe, s_load[k], g * 64 + 64, s_passed)
                    wait_alone(pe, s_xT, nxt, s_passed)
                    for b in range(B):
                        cols = slice((b % 4) * P, (b % 4 + 1) * P)
                        mm = pe.matmul(psX[0:D, k, b // 4, cols], kvs[:, b, :], q3Ts[:, k, b // 4, cols], start=True, stop=True)
                    mm.then_inc(s_out, 1)
                for k in range(K3):
                    nxt = g * K3 + (k + 1)
                    pe.wait_ge(s_ret, nxt)
                    if k == 2:
                        pe.wait_ge(s_pb, g * K3 + 1)
                    for b in range(B):
                        mm = pe.matmul(psV[0:P, k % 2, b * D:(b + 1) * D], x3Ts[:, k, b // 4, (b % 4) * P:(b % 4 + 1) * P],
                                       wp[:, :], start=True, stop=True)
                    mm.then_inc(s_proj, 1)
                for k in range(K3):
                    nxt = g * K3 + (k + 1)
                    wait_alone(pe, s_xn, nxt, s_passed)
                    for b in range(B):
                        mm = pe.transpose(psX[0:D, k, b // 4, (b % 4) * P:(b % 4 + 1) * P], xns[:, k, b, :], ident[0:P, 0:P])
                    mm.then_inc(s_xTp, 1)

        @block.scalar
        def _(act):
            act.sem_inc(s_xT, K3)
            with act.Fori(0, NI // K3) as g:
                for k in range(K3):
                    act.wait_ge(s_pb, g * K3 + (k + 1))
                    act.activation(ges[:, k], pbs[:, k], ACT.Gelu).then_inc(s_ge, 1)
                act.wait_ge(s_var, g + 1)
                act.activation(st[:, 2], st[:, 1], ACT.Sqrt).then_inc(s_std, 1)
                for k in range(K3):
                    nxt = g * K3 + (k + 1)
                    act.wait_ge(s_xTp, nxt)
                    for u in range(2):
                        ins = act.copy(xTs[:, k, u, :], psX[0:D, k, u, 0:HALF])
                    ins.then_inc(s_xT, 1)
                    act.wait_ge(s_xT, nxt + K3)
                    i = act.snap(g * K3 + k)
                    act.dma_start(d["h2"][i], hbs[:, k]).then_inc(s_store[k], 16)
                    act.dma_start(d["x4T"][:, 0:G * P].rearrange("o (i u n) -> i o u n", i=NI, u=2)[i], xTs[:, k]).then_inc(s_store[k], 16)
            for k in range(K3):
                act.wait_ge(s_store[k], 32 + 32 * (NI // K3))
            act.dma_start(d["x4T"][:, G * P:G * P + C3], xTs[:, 0, 0, 0:C3]).then_inc(s_store[0], 16)
            act.wait_ge(s_store[0], 48 + 32 * (NI // K3))

        @block.vector
        def _(dve):
            c = Chain(dve, s_dve)
            v = nc.vector
            dve.wait_ge(s_c, 64)
            v.tensor_tensor(kvs[:, :, :], kvs[:, :, :], headmask[:, :].unsqueeze(1).to_broadcast([D, B, D]),
                            ALU.mult).then_inc(s_kvm, 1)
            with dve.Fori(0, NI // K3) as g:
                for k in range(K3):
                    nxt = g * K3 + (k + 1)
                    dve.wait_ge(s_load[k], g * 64 + 64)
                    dve.wait_ge(s_out, nxt)
                    for u in range(2):
                        ins = v.tensor_tensor(x3Ts[:, k, u, :], x3Ts[:, k, u, :], psX[0:D, k, u, 0:HALF], ALU.add)
                    ins.then_inc(s_ret, 1)
                    c.send(v.tensor_tensor(hbs[:, k], hbs[:, k], x3s[:, k], ALU.add))
                c.join()
                for k in range(K3):
                    nxt = g * K3 + (k + 1)
                    dve.wait_ge(s_proj, nxt)
                    v.tensor_tensor(pbs[:, k], psV[0:P, k % 2, :].rearrange("p (b o) -> p b o", b=B),
                                    bp[:, :].unsqueeze(1).to_broadcast([P, B, D]), ALU.add).then_inc(s_pb, 1)
                for k in range(K3):
                    dve.wait_ge(s_ge, g * K3 + (k + 1))
                    c.send(v.tensor_tensor(hbs[:, k], hbs[:, k], ges[:, k], ALU.add))
                c.join()
                h, xn = hbs[:, :, :, :], xns[:, :, :, :]
                mean, var, std = st[:, 0], st[:, 1], st[:, 2]
                full = [P, K3, B, D]
                c(v.tensor_reduce(mean, h, AX_X, ALU.add))
                c(v.tensor_scalar(mean, mean, 1.0 / D, None, ALU.mult))
                c(v.tensor_tensor(xn, h, mean.unsqueeze(3).to_broadcast(full), ALU.subtract))
                c(v.tensor_tensor(sq[:, :, :, :], xn, xn, ALU.mult))
                c(v.tensor_reduce(var, sq[:, :, :, :], AX_X, ALU.add))
                v.tensor_scalar(var, var, 1.0 / D, EPS, ALU.mult, ALU.add).then_inc(s_var, 1)
                dve.wait_ge(s_std, g + 1)
                c(v.reciprocal(std, std))
                for k in range(K3):
                    v.tensor_tensor(xns[:, k], xns[:, k], st[:, 2, k].unsqueeze(2).to_broadcast([P, B, D]), ALU.mult).then_inc(s_xn, 1)
                c.restart()


KT = 32
LA = 4
UNITS_BEFORE = 16
UNITS_SEL = 10
UNITS = 32


FREE_AT = (2, 17, 22, 27)


def units_at(h, kt):
    if kt == 7:
        return [("kv", h)]
    if kt == 12:
        return [("keysT", h)]
    if kt not in FREE_AT:
        return []
    k = FREE_AT.index(kt)
    if h == 1:
        return [("query", k)]
    g = h // 6
    n = 4 * (h - (2, 6)[g]) + k
    if h in (2, 3, 6, 7) and n < 6:
        return [("score", n // 2, 2 * (n % 2) + g)]
    return []


FIRST_UNITS = [("query", k) for k in range(4)] + [("score", t, 2 * p + g) for g in range(2) for t in range(3) for p in range(2)]
LAST_UNITS = [("kv", 0), ("keysT", 0)]
STACK_AT = {4: 0, 9: 1, 14: 2}
ACT_BEHIND, DVE_BEHIND = 4, 3
PIECES = {1: "max0", 2: "max1", 4: "drop0", 5: "drop1", 7: "next0", 8: "next1", 10: "shift",
          12: "sums", 14: "smax", 15: "sdrop", 16: "snext", 18: "bound", 20: "parts", 27: "low", 29: "scale"}


def memory(nc, t, d, tab, s_tab):
    with ExitStack() as ctx:
        sb, ps, sem = pool_of(ctx, nc, "memory")
        ident, ident16 = sb("ident", [128, 128]), sb("ident16", [128, 128], F16)
        wqpk, pkeys = sb("wqpk", [D, 4, 128]), sb("pkeys", [128, 4, 4, NK])
        sel = sb("sel", [128, 2, 8, 128], F16)
        xT = sb("xT", [D, C3])
        qpk = sb("qpk", [128, 4, C3])
        sc = sb("sc", [P, 3, 2, H, NK])
        t16, tr = sb("t16", [P, 3, 2, TOPK]), sb("tr", [P, 3, 2, TOPK])
        tmp = sb("tmp", [P, 3, 2, NK])
        cand, ctmp = sb("cand", [P, 3, NCAND]), sb("ctmp", [P, 3, NCAND])
        c16, e16 = sb("c16", [P, 3, TOPK]), sb("e16", [P, 3, TOPK])
        thr = sb("thr", [P, 3, 3])
        rz = sb("rz", [P, 3])
        ab, lo32 = sb("ab", [P, 2, 3, NK]), sb("lo32", [P, 2, 3, NK])
        stk = sb("stk", [P, 2, 3, 5, 2, 32], F16)
        stack = sb("stack", [128, 2, 4, C3], F16)
        scale = sb("scale", [P, 4, 3])
        ew, ww = sb("ew", [128, 4, C3]), sb("ww", [128, 4, C3])
        kvT = sb("kvT", [128, C3])
        kvo = sb("kvo", [P, 2, 3, 2 * D])
        kT = sb("kT", [D, 2, C3])
        psS = ps("psS", [128, 4, 512])
        psKV = ps("psKV", [128, 2, 512])
        psT = ps("psT", [128, 4, 2, P], F16)
        psM = ps("psM", [128, 512])

        s_c, s_x, s_passed, s_id = sem("consts_in"), sem("chunk_in"), sem("waits_passed"), sem("ident16")
        s_sum, s_exp, s_weight = sem("sums"), sem("exps"), sem("weights")
        s_acc, s_kvT = sem("head_product"), sem("head_product_sb")
        s_unit, s_unit_used = sem("unit"), sem("unit_used")
        s_T, s_T_used = sem("stack_ps"), sem("stack_sb")
        s_sel_chain = sem("selection_chain")
        s_bound, s_ex, s_parts, s_hi, s_lo, s_stk = sem("bound"), sem("ex"), sem("parts"), sem("hi"), sem("lo"), sem("stk")
        s_kvo, s_kT = sem("kv_scaled"), sem("keysT_sb")
        s_stored = [sem("stored0"), sem("stored1")]
        block = ctx.enter_context(nc.Block())

        @block.sync
        def _(sp):
            def store(c, h):
                wait_alone(sp, s_kT, c * H + (h + 1), s_passed)
                k, w, ahead = (h - 1) % 2, (h - 1) % H, min(h, 1)
                sp.dma_start(d["KT"][w, :, ahead * C3:ahead * C3 + G * P].rearrange("o (c n) -> c o n", n=C3)[c]
                             if h or type(c) is not int else d["KT"][w, :, G * P:G * P + C3], kT[:, k, :]).then_inc(s_stored[k], 16)
                sp.dma_start(d["V"][w, 3 * ahead:3 * ahead + G].rearrange("(c t) p o -> c p t o", t=3)[c]
                             if h or type(c) is not int else d["V"][w, G:G + 3].rearrange("t p o -> p t o"),
                             kvo[:, k, :, D:2 * D]).then_inc(s_stored[k], 16)

            sp.dma_start(ident[:, :], t["ident"]).then_inc(s_c, 16)
            sp.dma_start(wqpk[:, :, :], t["wqpk"].rearrange("d (k n) -> d k n", k=4)).then_inc(s_c, 16)
            sp.dma_start(sel[:, :, :, :], t["sel"].rearrange("r (o s m) -> r o s m", o=2, s=8)).then_inc(s_c, 16)
            sp.dma_start(pkeys[:, :, :, :], t["pkeys"].rearrange("r (b k n) -> r b k n", b=4, k=4)).then_inc(s_c, 16)
            sp.dma_start(xT[:, :], d["x4T"][:, 0:C3]).then_inc(s_x, 16)
            for k in range(2):
                sp.sem_inc(s_stored[k], 32)
            sp.wait_ge(s_unit, 4)
            with sp.Fori(0, NC) as c:
                sp.dma_start(xT[:, :], d["x4T"].rearrange("o (c n) -> c o n", n=C3)[c + 1]).then_inc(s_x, 16)
                for h in range(H):
                    store(c, h)
            store(NC, 0)
            sp.wait_ge(s_stored[1], 32 + 32 * (NC * H // 2 + 1))
            sp.wait_ge(s_stored[0], 32 + 32 * NC * H // 2)

        @block.tensor
        def _(pe):
            def sums(c, n):
                h, kt = (n // KT) % H, n % KT
                v, q = kt // 8, kt % 8
                pe.matmul(psS[:, n % 4, 0:C3], sel[:, v % 2, q, :], stack[:, h % 2, v, :],
                          start=True, stop=True).then_inc(s_sum, 1)

            def unit(c, j, u):
                kind = u[0]
                pe.wait_ge(s_unit_used, c * UNITS + (UNITS_BEFORE + j))
                if kind == "query":
                    if type(c) is int:
                        pe.wait_ge(s_x, 16)
                    else:
                        pe.wait_ge(s_x, c * 16 + 32)
                    mm = pe.matmul(psM[:, 0:C3], wqpk[:, u[1], :], xT[:, :], start=True, stop=True)
                elif kind == "score":
                    _, ti, blk = u
                    mm = pe.matmul(psM[0:P, 0:4 * NK], qpk[:, blk, ti * P:(ti + 1) * P],
                                   pkeys[:, blk, :, :].rearrange("r k n -> r (k n)"), start=True, stop=True)
                elif kind == "kv":
                    wait_alone(pe, s_kvT, c * H + (u[1] + 2), s_passed)
                    for ti in range(3):
                        mm = pe.transpose(psM[0:P, ti * 128:(ti + 1) * 128], kvT[:, ti * P:(ti + 1) * P], ident[:, :])
                else:
                    wait_alone(pe, s_kvo, c * H + (u[1] + 1), s_passed)
                    for ti in range(3):
                        mm = pe.transpose(psM[0:D, ti * P:(ti + 1) * P], kvo[:, (u[1] + 1) % 2, ti, 0:D], ident[0:P, 0:P])
                mm.then_inc(s_unit, 1)

            def turn(c, h, ti):
                one = type(c) is int
                if ti == 0:
                    if one:
                        pe.wait_ge(s_stk, h + 1)
                    else:
                        wait_alone(pe, s_stk, c * H + (h + 1), s_passed)
                if one:
                    if ti:
                        pe.wait_ge(s_T_used, 3 * h + ti)
                else:
                    wait_alone(pe, s_T_used, c * (3 * H) + (3 * h + ti), s_passed)
                for v in range(4):
                    mm = pe.transpose(psT[:, v, 0, :], stk[:, h % 2, ti, v:v + 2, :, :].rearrange("p v w e -> p (v w e)"),
                                      ident16[0:P, 0:P])
                mm.then_inc(s_T, 1)

            pe.wait_ge(s_c, 16 * 4)
            for j, u in enumerate(FIRST_UNITS):
                unit(0, j - UNITS_BEFORE, u)
            pe.wait_ge(s_id, 1)
            for ti in range(3):
                turn(0, 0, ti)
            pe.wait_ge(s_T_used, 3)
            for n in range(LA):
                sums(0, n)
            pe.matmul(psKV[:, 1, 0:C3], wqpk[:, 0, :], wqpk[:, :, :].rearrange("d k n -> d (k n)")[:, 0:C3], start=True, stop=True).then_inc(s_acc, 1)
            pe.wait_ge(s_tab, 16 * H)
            with pe.Fori(0, NC) as c:
                j = 0
                for h in range(H):
                    for kt in range(KT):
                        n = h * KT + kt
                        if kt == 0:
                            pe.wait_ge(s_kvT, c * H + (h + 1))
                        pe.wait_ge(s_weight, c * (H * KT) + (n + 1))
                        mm = pe.matmul(psKV[:, h % 2, 0:C3], tab[h][:, kt, :], ww[:, n % 4, :],
                                       start=(kt == 0), stop=(kt == KT - 1))
                        if kt == KT - 1:
                            mm.then_inc(s_acc, 1)
                        if kt == KT - LA:
                            pe.wait_ge(s_T_used, c * (3 * H) + 3 * (h + 2))
                        sums(c, n + LA)
                        for u in units_at(h, kt):
                            unit(c, j, u)
                            j += 1
                        if kt in STACK_AT:
                            turn(c, h + 1, STACK_AT[kt])
                assert j == UNITS
            for j, u in enumerate(LAST_UNITS):
                unit(NC, j, u)

        @block.scalar
        def _(act):
            def unit(c, j, u):
                kind = u[0]
                one = type(c) is int
                if kind == "kv":
                    return
                act.wait_ge(s_unit, c * UNITS + (UNITS_BEFORE + j + 1))
                if kind == "query":
                    act.copy(qpk[:, u[1], :], psM[:, 0:C3]).then_inc(s_unit_used, 1)
                elif kind == "score":
                    _, ti, blk = u
                    if not one:
                        act.wait_ge(s_parts, c * H + 4 * (1 + blk % 2))
                    h0 = 4 * (blk % 2)
                    act.copy(sc[:, ti, blk // 2, h0:h0 + 4, :].rearrange("p h n -> p (h n)"), psM[0:P, 0:4 * NK]
                             ).then_inc(s_unit_used, 1)
                else:
                    h = u[1]
                    act.wait_ge(s_stored[(h + 1) % 2], c * (16 * H) + 32 * (h // 2 + 1))
                    act.copy(kT[:, (h + 1) % 2, :], psM[0:D, 0:C3]).then_inc(s_kT, 1)
                    act.wait_ge(s_kT, c * H + (h + 1))
                    act.sem_inc(s_unit_used, 1)

            def from_turn(c, h, ti):
                act.wait_ge(s_T, 3 * h + ti + 1 if type(c) is int else c * (3 * H) + (3 * h + ti + 1))
                act.copy(stack[:, h % 2, :, ti * P:(ti + 1) * P], psT[:, :, 0, :]).then_inc(s_T_used, 1)

            def at(c, s):
                return s + 1 if type(c) is int else c * H + (s + 1)

            def roots(c, s):
                act.wait_ge(s_bound, at(c, s))
                act.activation(e16[:, :, :], c16[:, :, :], ACT.Exp)
                act.activation(thr[:, 2, :], thr[:, 1, :], ACT.Exp).then_inc(s_ex, 1)

            def high(c, s):
                act.wait_ge(s_parts, at(c, s))
                for w in range(2):
                    ins = act.copy(stk[:, s % 2, :, w:w + 3:2, 0, :], ab[:, w, :, :].rearrange("p t (u e) -> p t u e", u=2))
                ins.then_inc(s_hi, 1)

            def low(c, s):
                act.wait_ge(s_lo, at(c, s))
                for w in range(2):
                    act.mul(stk[:, s % 2, :, w:w + 3:2, 1, :], lo32[:, w, :, :].rearrange("p t (u e) -> p t u e", u=2), 2048.0)
                src = ab[:, 0, :, 0:32]
                act.copy(stk[:, s % 2, :, 4, 0, :], src)
                act.mul(stk[:, s % 2, :, 4, 1, :], lo32[:, 0, :, 0:32], 2048.0).then_inc(s_stk, 1)

            act.sem_inc(s_kvT, 1)
            for s, some in enumerate((FIRST_UNITS[:UNITS_SEL], FIRST_UNITS[UNITS_SEL:])):
                for j, u in enumerate(some):
                    unit(0, s * UNITS_SEL + j - UNITS_BEFORE, u)
                roots(0, s)
                high(0, s)
                low(0, s)
            for ti in range(3):
                from_turn(0, 0, ti)
            with act.Fori(0, NC) as c:
                j = 0
                for h in range(H):
                    for kt in range(KT):
                        n = h * KT + kt
                        act.wait_ge(s_sum, c * (H * KT) + (n + 1))
                        act.activation(ew[:, n % 4, :], psS[:, n % 4, 0:C3], ACT.Exp).then_inc(s_exp, 1)
                        if kt == ACT_BEHIND + 1:
                            act.wait_ge(s_acc, c * H + (h + 1))
                            act.copy(kvT[:, :], psKV[:, (h - 1) % 2, 0:C3]).then_inc(s_kvT, 1)
                        for u in units_at(h, kt - ACT_BEHIND):
                            unit(c, j, u)
                            j += 1
                        if kt - ACT_BEHIND in STACK_AT:
                            from_turn(c, h + 1, STACK_AT[kt - ACT_BEHIND])
                        if kt == 23:
                            roots(c, h + 2)
                        if kt == 25:
                            high(c, h + 2)
                        if kt == 30:
                            low(c, h + 2)
            act.wait_ge(s_acc, NC * H + 1)
            act.copy(kvT[:, :], psKV[:, 1, 0:C3]).then_inc(s_kvT, 1)
            for j, u in enumerate(LAST_UNITS):
                unit(NC, j, u)

        @block.vector
        def _(dve):
            v = nc.vector
            ch = Chain(dve, s_sel_chain)

            def at(c, s):
                return s + 1 if type(c) is int else c * H + (s + 1)

            def piece(c, s, what):
                h = s % H
                one = type(c) is int
                rows = [(ti, w) for ti in range(3) for w in range(2)]
                ch.join()
                if what == "max0" and not one:
                    if s >= H:
                        wait_alone(dve, s_unit_used, c * UNITS + (UNITS_BEFORE + SCORES_A), s_passed)
                    elif s == 4:
                        wait_alone(dve, s_unit_used, c * UNITS + (UNITS_BEFORE + SCORES_B - UNITS), s_passed)
                if what in ("max0", "max1"):
                    for ti, w in rows[3 * int(what[-1]):][:3]:
                        ch.send(v.max(t16[:, ti, w, 0:8], sc[:, ti, w, h, :]))
                elif what in ("drop0", "drop1"):
                    for ti, w in rows[3 * int(what[-1]):][:3]:
                        ch.send(v.match_replace(tmp[:, ti, w, :], t16[:, ti, w, 0:8], sc[:, ti, w, h, :], -3.0e38))
                elif what in ("next0", "next1"):
                    for ti, w in rows[3 * int(what[-1]):][:3]:
                        ch.send(v.max(t16[:, ti, w, 8:16], tmp[:, ti, w, :]))
                elif what == "shift":
                    if not one:
                        wait_alone(dve, s_stk, c * H + s, s_passed)
                    elif s:
                        dve.wait_ge(s_stk, s)
                    for w in range(2):
                        top = t16[:, :, w, 0:1]
                        ch.send(v.tensor_tensor(tr[:, :, w, :], t16[:, :, w, :], top.to_broadcast([P, 3, TOPK]), ALU.subtract))
                        ch.send(v.tensor_tensor(ab[:, w, :, :], sc[:, :, w, h, :], top.to_broadcast([P, 3, NK]), ALU.subtract))
                elif what == "sums":
                    o = 0
                    for a, na, nb in CAND:
                        dst = cand[:, :, o:o + na * nb].rearrange("p t (a b) -> p t a b", a=na)
                        ch.send(v.tensor_tensor(dst, tr[:, :, 0, a:a + na].unsqueeze(3).to_broadcast([P, 3, na, nb]),
                                                tr[:, :, 1, 0:nb].unsqueeze(2).to_broadcast([P, 3, na, nb]), ALU.add))
                        o += na * nb
                elif what == "smax":
                    for ti in range(3):
                        ch.send(v.max(c16[:, ti, 0:8], cand[:, ti, :]))
                elif what == "sdrop":
                    for ti in range(3):
                        ch.send(v.match_replace(ctmp[:, ti, :], c16[:, ti, 0:8], cand[:, ti, :], -3.0e38))
                elif what == "snext":
                    for ti in range(3):
                        ch.send(v.max(c16[:, ti, 8:16], ctmp[:, ti, :]))
                elif what == "bound":
                    ch(v.tensor_scalar(thr[:, 0, :], c16[:, :, TOPK - 1], 1.0 + 2.0 ** -20, -(2.0 ** -16), ALU.mult, ALU.add))
                    ch(v.tensor_scalar(thr[:, 0, :], thr[:, 0, :], -104.0, None, ALU.max))
                    v.tensor_scalar(thr[:, 1, :], thr[:, 0, :], SHIFT, None, ALU.add).then_inc(s_bound, 1)
                    if one:
                        dve.wait_ge(s_bound, at(c, s))
                    else:
                        wait_alone(dve, s_bound, at(c, s), s_passed)
                elif what == "parts":
                    ch(v.tensor_tensor(ab[:, 0, :, :], ab[:, 0, :, :], thr[:, 1, :].unsqueeze(2).to_broadcast([P, 3, NK]), ALU.subtract))
                    if not one:
                        wait_alone(dve, s_T, c * (3 * H) + 3 * (s - 1), s_passed)
                    v.tensor_scalar(ab[:, :, :, :], ab[:, :, :, :], -30000.0, None, ALU.max).then_inc(s_parts, 1)
                elif what == "low":
                    if one:
                        dve.wait_ge(s_hi, at(c, s))
                    else:
                        wait_alone(dve, s_hi, at(c, s), s_passed)
                    for w in range(2):
                        ins = v.tensor_tensor(lo32[:, w, :, :].rearrange("p t (u e) -> p t u e", u=2),
                                              ab[:, w, :, :].rearrange("p t (u e) -> p t u e", u=2),
                                              stk[:, s % 2, :, w:w + 3:2, 0, :], ALU.subtract)
                    ins.then_inc(s_lo, 1)
                elif what == "scale":
                    if one:
                        dve.wait_ge(s_ex, at(c, s))
                    else:
                        wait_alone(dve, s_ex, at(c, s), s_passed)
                    ch(v.tensor_reduce(rz[:, :], e16[:, :, :], AX_X, ALU.add))
                    ch(v.reciprocal(rz[:, :], rz[:, :]))
                    ch.send(v.tensor_tensor(scale[:, s % 4, :], thr[:, 2, :], rz[:, :], ALU.mult))

            def unit(c, j, u):
                if u[0] != "kv":
                    return
                h = u[1]
                ch.join()
                dve.wait_ge(s_stored[(h + 1) % 2], c * (16 * H) + 32 * (h // 2 + 1))
                dve.wait_ge(s_unit, c * UNITS + (UNITS_BEFORE + j + 1))
                v.tensor_tensor(kvo[:, (h + 1) % 2, :, :], psM[0:P, 0:3 * 128].rearrange("p (t n) -> p t n", t=3),
                                scale[:, (h + 3) % 4, :].unsqueeze(2).to_broadcast([P, 3, 128]), ALU.mult).then_inc(s_kvo, 1)
                dve.wait_ge(s_kvo, c * H + (h + 1))
                dve.sem_inc(s_unit_used, 1)

            ch.send(v.memset(scale[:, :, :], 0.0))
            dve.wait_ge(s_c, 16 * 4)
            v.tensor_copy(ident16[:, :], ident[:, :]).then_inc(s_id, 1)
            dve.wait_ge(s_unit_used, UNITS_SEL)
            for s in range(2):
                for what in PIECES.values():
                    piece(0, s, what)
            ch.restart()
            with dve.Fori(0, NC) as c:
                j = 0
                for h in range(H):
                    for kt in range(KT):
                        n = h * KT + kt
                        dve.wait_ge(s_exp, c * (H * KT) + (n + 1))
                        v.scalar_tensor_tensor(ww[:, n % 4, :], psS[:, n % 4, 0:C3], -SHIFT, ew[:, n % 4, :],
                                               ALU.is_ge, ALU.mult).then_inc(s_weight, 1)
                        for u in units_at(h, kt - DVE_BEHIND):
                            unit(c, j, u)
                            j += 1
                        if kt in PIECES:
                            piece(c, h + 2, PIECES[kt])
                ch.restart()
            for j, u in enumerate(LAST_UNITS):
                unit(NC, j, u)


NU = NI * (NI // 3 + 1) // 2
ROW_UNITS = [(i, kc) for i in range(NI) for kc in range(i // 3 + 1)]
COL_UNITS = [(j, qc) for qc in range(NI // 3) for j in range(3 * qc + 3)]


LAST_OF_GROUP = [2, 8, NU - 1]


def attention_order():
    first = [("query", 0, k) for k in range(3)] + [("row", 0, u) for u in range(NU)]
    first += [("turn", 0, 0), ("turn", 0, 1), ("col", 0, 0), ("col", 0, 1)]
    o = []
    for h in range(H):
        rows = 0
        for u in range(NU):
            o.append(("pv", h, u))
            if u in LAST_OF_GROUP:
                o.append(("copy", h, LAST_OF_GROUP.index(u)))
            if u in (4, 10):
                o.append(("out", h, (4, 10).index(u)))
            if u == 1 and h:
                o.append(("out", h - 1, 2))
            o.append(("col", h + (u + 2) // NU, (u + 2) % NU))
            if u < 3:
                o.append(("query", h + 1, u))
            if u == 4:
                o.append(("turn", h, 2))
            while rows < min(NU, u * 6 // 5):
                o.append(("row", h + 1, rows))
                rows += 1
            if u in (8, 12):
                o.append(("turn", h + 1, (8, 12).index(u)))
    o.append(("out", H - 1, 2))
    return first, o


def misc_at(kind, h, u):
    if kind == "query":
        return u if h == 0 else 6 * h - 1 + u
    return 6 * h + 3 + u if u < 2 else 6 * (h + 1) + 2


def attention(nc, t, d, out):
    with ExitStack() as ctx:
        sb, ps, sem = pool_of(ctx, nc, "attn")
        NB = 4
        ident, ident_b = sb("ident", [128, 128]), sb("ident_b", [128, 128], BF16)
        causal, causal_b = sb("causal", [P, 2, P]), sb("causal_b", [P, 2, P], BF16)
        xb = sb("xb", [D, PAD])
        wq, wo = sb("wq", [D, NB, D]), sb("wo", [D + 1, NB, D + 1])
        kA, qA = sb("kA", [D + 1, NB, PAD]), sb("qA", [D + 1, 2, PAD])
        vA = sb("vA", [P, NB, NI, D + 1])
        mx, m3 = sb("mx", [P, NI, NI // 3]), sb("m3", [P, NI])
        nm = sb("nm", [P, NI, D + 1])
        ex = sb("ex", [P, 3, C3])
        oT = sb("oT", [D + 1, 2, C3])
        rz, yh = sb("rz", [P, 3]), sb("yh", [P, 3, D])
        y, res, final = sb("y", [P, NI, D]), sb("res", [P, NI, D]), sb("final", [P, NI, D])
        psA, psB, psO = ps("psA", [128, 2, 512]), ps("psB", [128, 2, 512]), ps("psO", [128, 2, 512])
        psM, psY = ps("psM", [128, 512]), ps("psY", [128, 512])
        s_c, s_set, s_bf, s_passed = sem("consts_in"), sem("buffers_set"), sem("bf16_set"), sem("waits_passed")
        s_in = [sem(f"head_in{k}") for k in range(NB)]
        s_pad, s_x, s_q, s_done = sem("pad_written"), sem("x_in"), sem("queries_made"), sem("head_done")
        s_misc, s_misc_used = sem("misc"), sem("misc_used")
        s_row, s_row_used, s_neg = sem("row"), sem("row_used"), sem("maxima")
        s_col, s_exp, s_pv = sem("col"), sem("exps"), sem("pv")
        s_oT, s_y, s_y_used = sem("oT"), sem("y"), sem("y_used")
        s_res, s_final, s_stored, s_chain = sem("residual_in"), sem("final"), sem("stored"), sem("dve_chain")
        block = ctx.enter_context(nc.Block())
        first, order = attention_order()
        N_U, N_3, N_M = H * NU, 3 * H, 6 * H

        @block.sync
        def _(sp):
            sp.sem_inc(s_done, NB)

            def load_x(b, ahead):
                src = d["x4T"][:, ahead * P:(ahead + G) * P].rearrange("o (i b p) -> b o i p", b=B, p=P)
                sp.dma_start(xb[:, :].rearrange("o (i p) -> o i p", p=P), src[b]).then_inc(s_x, 16)

            def load_head(b, ahead, h, w):
                kt = d["KT"][h, :, C3 + ahead * P:C3 + (ahead + G) * P].rearrange("o (i b p) -> b o i p", b=B, p=P)
                sp.dma_start(kA[0:D, w, :].rearrange("o (i p) -> o i p", p=P), kt[b]).then_inc(s_in[w], 16)
                vt = d["V"][h, 3 + ahead:3 + ahead + G].rearrange("(i b) p o -> b p i o", b=B)
                sp.dma_start(vA[:, w, :, 0:D], vt[b]).then_inc(s_in[w], 16)
                sp.dma_start(wq[:, w, :], t["wq"][h]).then_inc(s_in[w], 16)
                sp.dma_start(wo[0:D, w, 0:D], t["wo"][h]).then_inc(s_in[w], 16)

            load_x(0, 0)
            load_head(0, 0, 0, 0)
            sp.dma_start(ident[:, :], t["ident"]).then_inc(s_c, 16)
            sp.dma_start(causal[:, :, :], t["causal"]).then_inc(s_c, 16)
            sp.dma_start(d["KT"][0, :, C3 + G * P:], d["KT"][0, :, C3:C3 + P]).then_inc(s_pad, 16)
            sp.dma_start(d["V"][0, 3 + G:4 + G], d["V"][0, 3:4]).then_inc(s_pad, 16)
            sp.wait_ge(s_pad, 32)
            with sp.Fori(0, B) as b:
                for h in range(1, H + 1):
                    if h == H:
                        wait_alone(sp, s_q, b * H + H, s_passed)
                        load_x(b, 1)
                    wait_alone(sp, s_done, b * H + (h + 1), s_passed)
                    load_head(b, h // H, h % H, h % NB)

        @block.gpsimd
        def _(pool):
            v = nc.gpsimd
            set_one = Chain(pool, s_set)
            set_one(v.memset(kA[D:D + 1, :, :], 1.0))
            set_one(v.memset(vA[:, :, :, D:D + 1], 1.0))
            set_one(v.memset(nm[:, :, :], 0.0))
            set_one(v.memset(wo[0:D, :, D:D + 1], 0.0))
            set_one(v.memset(wo[D:D + 1, :, 0:D], 0.0))
            set_one(v.memset(wo[D:D + 1, :, D:D + 1], 1.0))
            with pool.Fori(0, B) as b:
                pool.dma_start(res[:, :, :], d["h2"].rearrange("i p b o -> b p i o")[b]).then_inc(s_res, 16)
                wait_alone(pool, s_final, b * 3 + 6, s_passed)
                pool.dma_start(out[b, 0:(NI - 1) * P, :].rearrange("(i p) o -> p i o", p=P), final[:, 0:NI - 1, :]).then_inc(s_stored, 16)
                pool.dma_start(out[b, (NI - 1) * P:SEQ, :], final[0:P - 1, NI - 1, :]).then_inc(s_stored, 16)
                wait_alone(pool, s_stored, b * 32 + 32, s_passed)

        @block.tensor
        def _(pe):
            pe.wait_ge(s_c, 32)
            pe.wait_ge(s_set, 6)
            pe.wait_ge(s_bf, 2)

            def steps(b, order):
                for kind, h, u in order:
                    k, w, n = h % 2, h % NB, h * NU + u
                    if kind in ("query", "turn"):
                        wait_alone(pe, s_misc_used, b * N_M + (misc_at(kind, h, u) + 1), s_passed)
                        if kind == "query":
                            if u == 0:
                                wait_alone(pe, s_x, b * 16 + 16 * (1 + h // H), s_passed)
                                wait_alone(pe, s_in[w], b * (64 * H // NB) + 64 * (h // NB + 1), s_passed)
                            mm = pe.matmul(psM[0:D, 0:C3], wq[:, w, :], xb[:, u * C3:(u + 1) * C3], start=True, stop=True)
                        else:
                            pe.wait_ge(s_neg, b * N_3 + (3 * h + u + 1))
                            for ti in range(3):
                                mm = pe.matmul(psM[0:D + 1, ti * P:(ti + 1) * P], nm[:, 3 * u + ti, :], ident[0:P, 0:P],
                                               start=True, stop=True)
                        mm.then_inc(s_misc, 1)
                    elif kind == "row":
                        i, kc = ROW_UNITS[u]
                        if u < 3 or u in (3, 9):
                            pe.wait_ge(s_misc_used, b * N_M + (misc_at("query", h, i // 3) + 2))
                        pe.wait_ge(s_row_used, b * N_U + (n + 1))
                        cols = min(3, i + 1 - 3 * kc) * P
                        diag = kc == i // 3
                        mm = pe.matmul(psA[0:P, n % 2, 0:cols], qA[0:D, k, i * P:(i + 1) * P],
                                       kA[0:D, w, kc * C3:kc * C3 + cols], start=True, stop=not diag)
                        if diag:
                            mm = pe.matmul(psA[0:P, n % 2, cols - P:cols], ident_b[0:P, 0:P], causal_b[:, 0, :],
                                           start=False, stop=True)
                        mm.then_inc(s_row, 1)
                    elif kind == "col":
                        j, qc = COL_UNITS[u]
                        if u in (0, 3, 9):
                            pe.wait_ge(s_misc_used, b * N_M + (misc_at("turn", h, qc) + 2))
                        pe.wait_ge(s_exp, b * N_U + (n + 1))
                        i0 = max(j, 3 * qc)
                        cols = (3 * qc + 3 - i0) * P
                        diag = j >= 3 * qc
                        mm = pe.matmul(psB[0:P, n % 2, 0:cols], kA[:, w, j * P:(j + 1) * P],
                                       qA[:, k, i0 * P:(3 * qc + 3) * P], start=True, stop=not diag)
                        if diag:
                            mm = pe.matmul(psB[0:P, n % 2, 0:P], ident_b[0:P, 0:P], causal_b[:, 1, :], start=False, stop=True)
                        mm.then_inc(s_col, 1)
                    elif kind == "pv":
                        j, qc = COL_UNITS[u]
                        m = 3 * h + qc
                        if j == 0:
                            pe.wait_ge(s_oT, b * N_3 + (m + 1))
                        pe.wait_ge(s_exp, b * N_U + (n + 3))
                        i0 = max(j, 3 * qc)
                        cols = (3 * qc + 3 - i0) * P
                        pe.matmul(psO[0:D + 1, m % 2, C3 - cols:C3], vA[:, w, j, :], ex[:, n % 3, 0:cols],
                                  start=(j == 0), stop=(j == 3 * qc + 2)).then_inc(s_pv, 1)
                    elif kind == "out":
                        m = 3 * h + u
                        pe.wait_ge(s_y_used, b * N_3 + (m + 1))
                        pe.wait_ge(s_oT, b * N_3 + (m + 3))
                        for ti in range(3):
                            mm = pe.matmul(psY[0:P, ti * (D + 1):(ti + 1) * (D + 1)], oT[:, m % 2, ti * P:(ti + 1) * P],
                                           wo[:, w, :], start=True, stop=True)
                        mm.then_inc(s_y, 1)

            steps(0, first)
            with pe.Fori(0, B) as b:
                steps(b, order)

        @block.scalar
        def _(act):
            act.sem_inc(s_exp, 2)
            act.sem_inc(s_misc_used, 1)
            act.sem_inc(s_oT, 2)

            def steps(b, order):
                for kind, h, u in order:
                    k, n = h % 2, h * NU + u
                    if kind == "query":
                        act.wait_ge(s_misc, b * N_M + (misc_at(kind, h, u) + 1))
                        act.mul(qA[0:D, k, u * C3:(u + 1) * C3], psM[0:D, 0:C3], D ** -0.5).then_inc(s_misc_used, 1)
                        if u == 2:
                            act.sem_inc(s_q, 1)
                    elif kind == "turn":
                        act.wait_ge(s_misc, b * N_M + (misc_at(kind, h, u) + 1))
                        act.copy(qA[D:D + 1, k, u * C3:(u + 1) * C3], psM[D:D + 1, 0:C3]).then_inc(s_misc_used, 1)
                    elif kind == "col":
                        j, qc = COL_UNITS[u]
                        cols = (3 * qc + 3 - max(j, 3 * qc)) * P
                        act.wait_ge(s_col, b * N_U + (n + 1))
                        act.wait_ge(s_pv, b * N_U + (n + 1))
                        act.activation(ex[:, n % 3, 0:cols], psB[0:P, n % 2, 0:cols], ACT.Exp).then_inc(s_exp, 1)
                    elif kind == "copy":
                        m = 3 * h + u
                        act.wait_ge(s_pv, b * N_U + (h * NU + LAST_OF_GROUP[u] + 4))
                        act.wait_ge(s_y, b * N_3 + (m + 1))
                        act.copy(oT[:, m % 2, :], psO[0:D + 1, m % 2, 0:C3]).then_inc(s_oT, 1)

            steps(0, first)
            with act.Fori(0, B) as b:
                steps(b, order)

        @block.vector
        def _(dve):
            c = Chain(dve, s_chain)
            v = nc.vector
            dve.wait_ge(s_c, 32)
            v.tensor_copy(ident_b[:, :], ident[:, :]).then_inc(s_bf, 1)
            v.tensor_copy(causal_b[:, :, :], causal[:, :, :]).then_inc(s_bf, 1)
            dve.sem_inc(s_row_used, 2)
            dve.sem_inc(s_y_used, 1)
            dve.sem_inc(s_pv, 3)
            dve.sem_inc(s_y, 2)
            dve.sem_inc(s_final, 3)

            def steps(b, order):
                for kind, h, u in order:
                    k, n = h % 2, h * NU + u
                    if kind == "row":
                        i, kc = ROW_UNITS[u]
                        cols = min(3, i + 1 - 3 * kc) * P
                        dve.wait_ge(s_row, b * N_U + (n + 1))
                        v.tensor_reduce(mx[:, i, kc:kc + 1], psA[0:P, n % 2, 0:cols], AX_X, ALU.max).then_inc(s_row_used, 1)
                        if i % 3 == 2 and kc == i // 3:
                            r = i // 3
                            tiles = slice(3 * r, 3 * r + 3)
                            dve.wait_ge(s_row_used, b * N_U + (n + 3))
                            c(v.tensor_reduce(m3[:, tiles], mx[:, tiles, 0:r + 1], AX_X, ALU.max))
                            if h:
                                dve.wait_ge(s_misc, b * N_M + (misc_at("turn", h - 1, r) + 1))
                            v.tensor_scalar(nm[:, tiles, D], m3[:, tiles], -1.0, None, ALU.mult).then_inc(s_neg, 1)
                    elif kind == "out":
                        m = 3 * h + u
                        tiles = slice(3 * u, 3 * u + 3)
                        dve.wait_ge(s_y, b * N_3 + (m + 3))
                        yv = psY[0:P, 0:3 * (D + 1)].rearrange("p (t e) -> p t e", t=3)
                        c(v.reciprocal(rz[:, :], yv[:, :, D]))
                        if h == 0:
                            dve.wait_ge(s_final, b * 3 + (u + 1))
                        v.tensor_tensor((yh[:, :, :] if h else y[:, tiles, :]), yv[:, :, 0:D],
                                        rz[:, :].unsqueeze(2).to_broadcast([P, 3, D]), ALU.mult).then_inc(s_y_used, 1)
                        dve.wait_ge(s_y_used, b * N_3 + (m + 2))
                        if h:
                            c(v.tensor_tensor(y[:, tiles, :], y[:, tiles, :], yh[:, :, :], ALU.add))
                        if h == H - 1:
                            dve.wait_ge(s_res, b * 16 + 16)
                            v.tensor_tensor(final[:, tiles, :], y[:, tiles, :], res[:, tiles, :], ALU.add).then_inc(s_final, 1)
                        if u == 2:
                            dve.sem_inc(s_done, 1)

            steps(0, first)
            c.restart()
            with dve.Fori(0, B) as b:
                steps(b, order)
                c.restart()


def count_units():
    n, last = 0, {}
    for h in range(H):
        for kt in range(KT):
            for u in units_at(h, kt):
                n += 1
                if u[0] == "score":
                    last[u[2] % 2] = n
    return last[0], last[1]


SCORES_A, SCORES_B = count_units()


def lay_out(a):
    def c(x):
        return np.ascontiguousarray(x)

    o = {}
    o["x"] = lay_out_x(a["x"])
    o["cls_tok"] = c(a["cls_tok"][0])
    o["L0_tok_W"] = c(a["L0_tok_W"].reshape(D, 2, PATCH // 2 + 1, C_IN).transpose(1, 2, 3, 0).reshape(18, C_IN * D))
    eo = np.concatenate([np.arange(0, D, 2), np.arange(1, D, 2)])
    o["wqk"] = c(np.concatenate([a["L0_attn_W_Q"][:, eo], a["L0_attn_W_K"][:, eo]], 1))
    o["wv"] = c(a["L0_attn_W_V"])
    o["gate_w"], o["gate_b"] = c(a["L0_ffn_gate_w"]), c(a["L0_ffn_gate_b"][None])
    o["w1"], o["b1"] = c(a["L0_ffn_w1"].transpose(1, 0, 2)), c(a["L0_ffn_b1"].T)
    o["w2"], o["b2"] = c(a["L0_ffn_w2"].transpose(1, 0, 2)), c(a["L0_ffn_b2"])
    o["ln_g"], o["ln_b"] = c(a["L0_ffn_gamma"][None]), c(a["L0_ffn_beta"][None])
    w = a["L1_attn_W_qkv"].reshape(16, 3, 4, D)
    bq = a["L1_attn_b_qkv"].reshape(16, 3, 4)
    o["wq3"] = c(w[:, 0].reshape(D, D).T)
    o["wkv3"] = c(w[:, 1:].transpose(1, 0, 2, 3).reshape(2 * D, D).T)
    o["bq3"] = c(bq[:, 0].reshape(D, 1))
    o["bkv3"] = c(bq[:, 1:].transpose(1, 0, 2).reshape(1, 2 * D))
    for k, n in (("hln_w", "w"), ("hln_b", "b")):
        o[k] = c(np.concatenate([a["L1_attn_kln_" + n].reshape(1, D), a["L1_attn_vln_" + n].reshape(1, D)], 1))
    o["wp3"], o["bp3"] = c(a["L1_attn_W_proj"].T), c(a["L1_attn_b_proj"][None])
    o["wqpk"] = c(a["L1_ffn_Wq_pk"])
    keys = a["L1_ffn_pk_keys"].reshape(2, NK, 2, 4, 32)
    blocks = np.zeros((4, 32, 2, 2, 4, NK), keys.dtype)
    for k in range(4):
        blocks[k, :, :, :, k, :] = keys[:, :, :, k, :].transpose(3, 0, 2, 1)
    o["pkeys"] = c(blocks.reshape(128, 16 * NK))
    o["wq"] = c(a["L1_ffn_Wq"].reshape(D, H, D).transpose(1, 0, 2))
    o["wo"] = c(a["L1_ffn_Wo"].reshape(H, D, D))
    tab = np.concatenate([a["L1_ffn_keys_table"], a["L1_ffn_values_table"]], 1)
    tab = tab.reshape(H, 2, 8, 4, 2, 32, 2 * D)
    tab = np.stack([tab[:, 0, :, :, 0], tab[:, 0, :, :, 1], tab[:, 1, :, :, 1], tab[:, 1, :, :, 0]], 1)
    o["table"] = c(tab.transpose(3, 4, 0, 1, 2, 5).reshape(128, H, KT, 2 * D))
    return o


def build(nc, t, out):
    d = {}
    for name, shape in (("gw", [PATCH, C_IN * D]), ("h0", [B, PAD + P, D]), ("h1", [NI, P, B, D]), ("x3", [NI, P, B, D]),
                        ("x3T", [NI, D, 2, HALF]), ("q3T", [NI, D, 2, HALF]), ("h2", [NI, P, B, D]),
                        ("x4T", [D, (NC + 1) * C3]), ("KT", [H, D, (G + 4) * P]), ("V", [H, G + 4, P, D])):
        d[name] = nc.dram_tensor("scratch_" + name, shape, F32, kind="Internal").ap()
    with ExitStack() as ctx:
        kvs = ctx.enter_context(nc.sbuf_tensor("kv_sums", [D, B, D], F32))
        tab = [ctx.enter_context(nc.sbuf_tensor(f"table{h}", [128, KT, 2 * D], F32)) for h in range(H)]
        s_tab = ctx.enter_context(nc.semaphore("table_in"))
        embed(nc, t, d)
        layer0_and_kv(nc, t, d, kvs, tab, s_tab)
        linear_attention(nc, t, d, kvs)
        memory(nc, t, d, tab, s_tab)
    attention(nc, t, d, out)


def kernel(**inputs):
    from concourse import bacc, bass_utils

    arrays = {**lay_out({k: np.asarray(v) for k, v in inputs.items()}), **constants()}
    nc = bacc.Bacc("TRN2", target_bir_lowering=False, num_devices=1)
    t = {k: nc.dram_tensor(f"in_{k}_dram", a.shape, mybir.dt.from_np(a.dtype), kind="ExternalInput").ap()
         for k, a in arrays.items()}
    out = nc.dram_tensor("out_dram", (B, SEQ, D), F32, kind="ExternalOutput").ap()
    build(nc, t, out)
    result = bass_utils.run_bass_kernel_spmd(nc, [{f"in_{k}_dram": a for k, a in arrays.items()}], core_ids=[0])
    return result.results[0]["out_dram"]
```
